# Optimizing a Trainium2 kernel written in Bass

```python
import numpy as np
import jax
import jax.numpy as jnp

def _softmax(x, axis=-1):
    return jax.nn.softmax(x, axis=axis)

def _gelu(x):
    return jax.nn.gelu(x, approximate=True)

def _silu(x):
    return jax.nn.silu(x)

def _sigmoid(x):
    return jax.nn.sigmoid(x)

def _layernorm(x, axis=-1, eps=1e-05):
    m = jnp.mean(x, axis=axis, keepdims=True)
    v = jnp.var(x, axis=axis, keepdims=True)
    return (x - m) / jnp.sqrt(v + eps)

def _scatter_add(tgt, idx, src, axis=0):
    return tgt.at[idx].add(src)

def _segment_sum(src, seg, n):
    return jax.ops.segment_sum(src, seg, n)
kernel_name = 'mk_gnn_preln_d2_gnn_r32_6c91e0'

def setup_inputs(seed: int=0):
    np.random.seed(seed)
    _w = jnp.asarray

    def _rec_inputs():
        import jax
        import jax.numpy as jnp
        _gk = jax.random.key(seed)
        x = -0.0003713 + 1 * jax.random.normal(jax.random.fold_in(_gk, 1), (50000, 128), jnp.float32)
        src = jax.random.randint(jax.random.fold_in(_gk, 2), (50000,), 0, 50000, jnp.int32)
        dst = jnp.minimum((50000 * jax.random.uniform(jax.random.fold_in(_gk, 3), (50000,)) ** 2.0).astype(jnp.int32), 49999)
        _o = jnp.argsort(dst, stable=True)
        src = src[_o]
        dst = dst[_o]
        edge_type_2 = jax.random.randint(jax.random.fold_in(_gk, 12), (50000,), 0, 2, jnp.int32)
        return (x, src, dst, edge_type_2)
    x, src, dst, edge_type_2 = _rec_inputs()

    def _L0_gnn_setup():
        import jax, jax.numpy as jnp
        import numpy as np
        N_NODES = 3125
        N_EDGES = 50000

        def _sage_conv(x, src, dst, Wl, b, Wr, n_nodes):
            msgs = x[src]
            agg = jax.ops.segment_sum(msgs, dst, num_segments=n_nodes)
            deg = jax.ops.segment_sum(jnp.ones((src.shape[0],), x.dtype), dst, num_segments=n_nodes)
            agg = agg / jnp.maximum(deg, 1.0)[:, None]
            return agg @ Wl + b + x @ Wr
        key = jax.random.key(seed)
        ks = jax.random.split(key, 8)
        x = jax.random.normal(ks[0], (N_NODES, 128), dtype=jnp.float32)
        edge_index = jax.random.randint(ks[1], (2, N_EDGES), 0, N_NODES, dtype=jnp.int64)

        def lin(k, din, dout):
            return jax.random.normal(k, (din, dout), dtype=jnp.float32) * (1.0 / np.sqrt(din))
        return {'x': x, 'edge_index': edge_index, 'Wl0': lin(ks[2], 128, 256), 'b0': jnp.zeros((256,), jnp.float32), 'Wr0': lin(ks[3], 128, 256), 'Wl1': lin(ks[4], 256, 256), 'b1': jnp.zeros((256,), jnp.float32), 'Wr1': lin(ks[5], 256, 256), 'Wl2': lin(ks[6], 256, 128), 'b2': jnp.zeros((128,), jnp.float32), 'Wr2': lin(ks[7], 256, 128)}
    _L0_gnn_all = _L0_gnn_setup()
    _L0_gnn_in = {k: v for k, v in _L0_gnn_all.items() if k in ('Wl0', 'b0', 'Wr0', 'Wl1', 'b1', 'Wr1', 'Wl2', 'b2', 'Wr2')}
    del _L0_gnn_all

    def _L1_gnn_setup():
        import jax, jax.numpy as jnp
        import numpy as np
        IN_DIM = 128
        OUT_DIM = 128
        N_NODES = 10000
        N_EDGES = 20000
        key = jax.random.key(seed)
        ks = jax.random.split(key, 9)
        X = jax.random.normal(ks[0], (N_NODES, IN_DIM), dtype=jnp.float32)
        edge_index = jax.random.randint(ks[1], (2, N_EDGES), 0, N_NODES, dtype=jnp.int64)
        edge_types = jax.random.randint(ks[2], (N_EDGES,), 0, 2, dtype=jnp.int64)
        s = 1.0 / np.sqrt(IN_DIM)
        W_data = jax.random.uniform(ks[3], (OUT_DIM, IN_DIM), minval=-s, maxval=s, dtype=jnp.float32)
        b_data = jax.random.uniform(ks[4], (OUT_DIM,), minval=-s, maxval=s, dtype=jnp.float32)
        W_control = jax.random.uniform(ks[5], (OUT_DIM, IN_DIM), minval=-s, maxval=s, dtype=jnp.float32)
        b_control = jax.random.uniform(ks[6], (OUT_DIM,), minval=-s, maxval=s, dtype=jnp.float32)
        W_self = jax.random.uniform(ks[7], (OUT_DIM, IN_DIM), minval=-s, maxval=s, dtype=jnp.float32)
        b_self = jax.random.uniform(ks[8], (OUT_DIM,), minval=-s, maxval=s, dtype=jnp.float32)
        return {'X': X, 'edge_index': edge_index, 'edge_types': edge_types, 'W_data': W_data, 'b_data': b_data, 'W_control': W_control, 'b_control': b_control, 'W_self': W_self, 'b_self': b_self}
    _L1_gnn_all = _L1_gnn_setup()
    _L1_gnn_in = {k: v for k, v in _L1_gnn_all.items() if k in ('W_data', 'b_data', 'W_control', 'b_control', 'W_self', 'b_self')}
    del _L1_gnn_all
    return {'x': x, 'src': src, 'dst': dst, 'edge_type_2': edge_type_2, 'L0_gnn_Wl0': _L0_gnn_in['Wl0'], 'L0_gnn_b0': _L0_gnn_in['b0'], 'L0_gnn_Wr0': _L0_gnn_in['Wr0'], 'L0_gnn_Wl1': _L0_gnn_in['Wl1'], 'L0_gnn_b1': _L0_gnn_in['b1'], 'L0_gnn_Wr1': _L0_gnn_in['Wr1'], 'L0_gnn_Wl2': _L0_gnn_in['Wl2'], 'L0_gnn_b2': _L0_gnn_in['b2'], 'L0_gnn_Wr2': _L0_gnn_in['Wr2'], 'L1_gnn_W_data': _L1_gnn_in['W_data'], 'L1_gnn_b_data': _L1_gnn_in['b_data'], 'L1_gnn_W_control': _L1_gnn_in['W_control'], 'L1_gnn_b_control': _L1_gnn_in['b_control'], 'L1_gnn_W_self': _L1_gnn_in['W_self'], 'L1_gnn_b_self': _L1_gnn_in['b_self']}

def reference(x, src, dst, edge_type_2, L0_gnn_Wl0, L0_gnn_b0, L0_gnn_Wr0, L0_gnn_Wl1, L0_gnn_b1, L0_gnn_Wr1, L0_gnn_Wl2, L0_gnn_b2, L0_gnn_Wr2, L1_gnn_W_data, L1_gnn_b_data, L1_gnn_W_control, L1_gnn_b_control, L1_gnn_W_self, L1_gnn_b_self):
    import jax
    import jax.numpy as jnp

    def _L0_gnn_ref(x, edge_index, Wl0, b0, Wr0, Wl1, b1, Wr1, Wl2, b2, Wr2):
        import jax, jax.numpy as jnp
        import numpy as np
        N_NODES = 3125
        N_EDGES = 50000

        def _sage_conv(x, src, dst, Wl, b, Wr, n_nodes):
            msgs = x[src]
            agg = jax.ops.segment_sum(msgs, dst, num_segments=n_nodes)
            deg = jax.ops.segment_sum(jnp.ones((src.shape[0],), x.dtype), dst, num_segments=n_nodes)
            agg = agg / jnp.maximum(deg, 1.0)[:, None]
            return agg @ Wl + b + x @ Wr
        src, dst = (edge_index[0], edge_index[1])
        n = x.shape[0]
        h = jax.nn.relu(_sage_conv(x, src, dst, Wl0, b0, Wr0, n))
        h = jax.nn.relu(_sage_conv(h, src, dst, Wl1, b1, Wr1, n))
        return _sage_conv(h, src, dst, Wl2, b2, Wr2, n)

    def _L1_gnn_ref(X, edge_index, edge_types, W_data, b_data, W_control, b_control, W_self, b_self):
        import jax, jax.numpy as jnp
        import numpy as np
        IN_DIM = 128
        OUT_DIM = 128
        N_NODES = 10000
        N_EDGES = 20000
        src, dst = (edge_index[0], edge_index[1])
        Xs = X[src]
        m_data = Xs @ W_data.T + b_data
        m_ctrl = Xs @ W_control.T + b_control
        msg = jnp.where((edge_types == 0)[:, None], m_data, m_ctrl)
        agg = jax.ops.segment_sum(msg, dst, num_segments=X.shape[0])
        out = agg + (X @ W_self.T + b_self)
        return jax.nn.relu(out)
    edge_index = jnp.stack([src, dst])
    h = jnp.maximum(_layernorm(x, axis=-1), 0.0)
    x = x + _L0_gnn_ref(h, edge_index, L0_gnn_Wl0, L0_gnn_b0, L0_gnn_Wr0, L0_gnn_Wl1, L0_gnn_b1, L0_gnn_Wr1, L0_gnn_Wl2, L0_gnn_b2, L0_gnn_Wr2)
    h = jnp.maximum(_layernorm(x, axis=-1), 0.0)
    x = x + _L1_gnn_ref(h, edge_index, edge_type_2, L1_gnn_W_data, L1_gnn_b_data, L1_gnn_W_control, L1_gnn_b_control, L1_gnn_W_self, L1_gnn_b_self)
    return x

_drawn_inputs = setup_inputs


def setup_inputs(seed=0):
    import zlib

    import numpy as np

    out = dict(_drawn_inputs(seed))
    spreads = {'L0_gnn_b0': (0.0, 0.1), 'L0_gnn_b1': (0.0, 0.1), 'L0_gnn_b2': (0.0, 0.1)}
    factors = {}
    for name, (base, spread) in spreads.items():
        noise = np.random.default_rng([zlib.crc32(name.encode()), seed]).standard_normal(out[name].shape)
        drawn = base * np.exp(spread * noise) if base else spread * noise
        out[name] = jnp.asarray(drawn.astype(out[name].dtype))
    for name, factor in factors.items():
        out[name] = (out[name] * factor).astype(out[name].dtype)
    return out
```

```python
from contextlib import ExitStack

import concourse.bass as bass
from concourse import mybir

ALU = mybir.AluOpType
ACT = mybir.ActivationFunctionType
F32 = mybir.dt.float32
F32R = mybir.dt.float32r
I32 = mybir.dt.int32

P = 128
U = 4
BLK = P * U
R = 4
EPS = 1e-5
PAD_DST = 1 << 20


def peeled_loop(eng, n, body):
    body(0)
    body(1)
    with eng.Fori(2, n - 1) as i:
        body(i)
    body(n - 1)


def wait(eng, sem, value):
    if isinstance(value, int) and value <= 0:
        return
    eng.wait_ge(sem, value)


def build(nc, x, src, dst, etype, Wl0, b0, Wr0, Wl1, b1, Wr1, Wl2, b2, Wr2,
          Wd, bd, Wc, bc, Ws, bs, out):
    N, D = x.shape
    E = src.shape[0]
    H = Wl0.shape[1]
    K = H // P
    NI = -(-max(N, E) // (R * BLK))
    NB = NI * R
    NP = NB * BLK
    FULL = N // BLK
    TAIL = (N - FULL * BLK) // U
    E_FULL = E // BLK
    assert D == P and H == 2 * P and TAIL * U == N - FULL * BLK
    assert (NI - 1) * R <= FULL
    ZROW = NP

    def dram(name, shape, dt=F32):
        return nc.dram_tensor(name, shape, dt, kind="Internal").ap()

    h0_t = dram("h0_t", (NP, D))
    h1_t = dram("h1_t", (NP, H))
    g2_t = dram("g2_t", (NP, D))
    s2_t = dram("s2_t", (NP, D))
    x1_t = dram("x1_t", (NP, D))
    self_t = dram("self_t", (NP, D))
    y_t = dram("y_t", (2 * NP, D))
    pa_t = dram("pa_t", (NP + P, D))
    pb_t = dram("pb_t", (NP + P, H))
    node_t = dram("node_t", (NP, 2))

    def rows_of(t, b):
        return t[at(b, BLK), :].rearrange("(p u) d -> p (u d)", u=U)

    def at(b, size=1):
        return bass.ds(b * size, size)

    def lagged(eng, *stages):
        def body(i):
            for s in range(R):
                for k, stage_k in enumerate(stages):
                    b = R * i + s - k
                    if stage_k is None or isinstance(b, int) and b < 0:
                        continue
                    q = (s - k) % R
                    stage_k(b, q, i - (q - s + k) // R)

        peeled_loop(eng, NI, body)
        for n in range(1, len(stages)):
            for k in range(n, len(stages)):
                b = NB - 1 + n - k
                if stages[k] is not None:
                    stages[k](b, b % R, b // R)

    def uses(s, i):
        return 2 * i + s // 2

    def load_x(sp, tile, b, s, c, done):
        if isinstance(b, int) and b == FULL:
            sp.dma_start(tile[0:TAIL, s, c:c + U * D], x[b * BLK:N, :].rearrange("(p u) d -> p (u d)", u=U))\
                .then_inc(done, 16)
        else:
            b = 0 if isinstance(b, int) and b > FULL else b
            sp.dma_start(tile[:, s, c:c + U * D], rows_of(x, b)).then_inc(done, 16)

    def accumulate(pe, o, products):
        for n, (lhsT, rhs) in enumerate(products):
            mm = pe.matmul(o, lhsT, rhs, start=(n == 0), stop=(n == len(products) - 1))
        return mm

    with ExitStack() as ctx:
        def sb(name, shape, dt=F32):
            return ctx.enter_context(nc.sbuf_tensor(name, shape, dt))

        phase = []

        def sem(name):
            return phase[0].enter_context(nc.semaphore(name))

        def run(make_phase, *args):
            with ExitStack() as semaphores:
                phase[:] = [semaphores]
                make_phase(*args)

        gathered = [ctx.enter_context(nc.semaphore(f"gathered{s}")) for s in range(R)]
        staged = ctx.enter_context(nc.semaphore("staged"))

        def gathers(nth, i):
            return 16 * U * (NI * nth + i)

        bank = [ctx.enter_context(nc.psum_tensor(f"bank{i}", [P, 512], F32)) for i in range(8)]

        ident = sb("ident", [P, P])
        ones = sb("ones", [P, P])
        iota_f = sb("iota_f", [P, P])
        slot_T = sb("slot_T", [P, NB, U])
        src_T = sb("src_T", [P, NB, U], I32)
        srcy_T = sb("srcy_T", [P, NB, U], I32)
        M = sb("M", [NB, U, U, NB])
        tlast_i = sb("tlast_i", [NB, U], I32)
        node_row = sb("node_row", [P, NB, U], I32)
        node_inv = sb("node_inv", [P, NB, U])
        W0h = sb("W0h", [P, 2, H], F32R)
        W0l = sb("W0l", [P, 2, H], F32R)
        W1h = sb("W1h", [P, 2, K, H], F32R)
        W1l = sb("W1l", [P, 2, K, H], F32R)
        W2h = sb("W2h", [P, K, 2 * D], F32R)
        W2l = sb("W2l", [P, K, 2 * D], F32R)
        W3h = sb("W3h", [P, 3 * D], F32R)
        W3l = sb("W3l", [P, 3 * D], F32R)
        bias0 = sb("bias0", [2, H], F32R)
        bias3 = sb("bias3", [2, 3 * D], F32R)
        ones_r = sb("ones_r", [2, P], F32R)
        b1_c = sb("b1_c", [P, K])
        b2_bc = sb("b2_bc", [P, U, D])
        sidx_T = sb("sidx_T", [P, NB, U], I32)
        payload_T = sb("payload_T", [P, NB, U, 2])
        zp = sb("zp", [P, 1])
        eps_c = sb("eps_c", [P, 1])

        def prepare(scratch):
            def sb(name, shape, dt=F32):
                return scratch.enter_context(nc.sbuf_tensor(name, shape, dt))

            dst_i = sb("dst_i", [NB, BLK], I32)
            next_i = sb("next_i", [NB, BLK], I32)
            src_i = sb("src_i", [NB, BLK], I32)
            typ_i = sb("typ_i", [NB, BLK], I32)
            dst_f = sb("dst_f", [NB, U, P])
            next_f = sb("next_f", [NB, U, P])
            src_f = sb("src_f", [NB, U, P])
            typ_f = sb("typ_f", [NB, U, P])
            pos = sb("pos", [NB, U, P])
            rbase = sb("rbase", [NB, U, P])
            e_idx = sb("e_idx", [NB, U, NB])
            k_idx = sb("k_idx", [NB, U])
            same = sb("same", [NB, U, P])
            starts = sb("starts", [NB, U, P])
            slot = sb("slot", [NB, U, P])
            row = sb("row", [NB, U, P])
            count = sb("count", [NB, U, P])
            first_run = sb("first_run", [NB, U, P])
            sidx = sb("sidx", [NB, U, P])
            srcy = sb("srcy", [NB, U, P])
            last_count = sb("last_count", [NB, U])
            diag = sb("diag", [NB, U, NB])
            hit = sb("hit", [NB, U, NB])
            zeros = sb("zeros", [P, H])
            fill = sb("fill", [P, NP // P, 2])
            w0 = sb("w0", [P, 2, H])
            w1 = sb("w1", [P, 2, K, H])
            w2 = sb("w2", [P, K, 2 * D])
            w3 = sb("w3", [P, 3 * D])
            bias0_f = sb("bias0_f", [2, H])
            bias3_f = sb("bias3_f", [2, 3 * D])
            bias0_h = sb("bias0_h", [2, H], F32R)
            bias3_h = sb("bias3_h", [2, 3 * D], F32R)
            bias0_l = sb("bias0_l", [2, H])
            bias3_l = sb("bias3_l", [2, 3 * D])

            consts = sem("pr_consts")
            pads = sem("pr_pads")
            rows_in = sem("pr_rows_in")
            w_in = sem("pr_w_in")
            filled = sem("pr_filled")
            eye = sem("pr_eye")
            step = sem("pr_step")
            diag_ready = sem("pr_diag_ready")
            bc_ready = sem("pr_bc_ready")
            m_ready = sem("pr_m_ready")
            carry_ready = sem("pr_carry_ready")
            arrays_ready = sem("pr_arrays_ready")
            turned = sem("pr_turned")
            w3_turned = sem("pr_w3_turned")
            w_hi = sem("pr_w_hi")

            row_loads = [(dst_i, dst, 0), (next_i, dst, 1), (src_i, src, 0), (typ_i, etype, 0)]
            whole = E_FULL * BLK
            with nc.Block() as block:

                @block.gpsimd
                def _(pool):
                    pool.memset(dst_i[:, :], PAD_DST).then_inc(pads, 1)
                    pool.memset(next_i[:, :], PAD_DST).then_inc(pads, 1)
                    pool.memset(src_i[:, :], 0).then_inc(pads, 1)
                    pool.memset(typ_i[:, :], 0).then_inc(pads, 1)
                    pool.memset(zeros[:, :], 0.0).then_inc(consts, 1)
                    pool.memset(fill[:, :, 0], float(ZROW)).then_inc(consts, 1)
                    pool.memset(fill[:, :, 1], 1.0).then_inc(consts, 1)
                    pool.memset(ident[:, :], 0.0).then_inc(eye, 1)
                    pool.memset(ones[:, :], 1.0).then_inc(consts, 1)
                    pool.memset(eps_c[:, :], EPS).then_inc(consts, 1)
                    pool.wait_ge(eye, 1)
                    pool.affine_select(out=ident[:, :], in_=ident[:, :], compare_op=ALU.not_equal, fill=1.0,
                                       base=0, pattern=[[-1, P]], channel_multiplier=1).then_inc(consts, 1)
                    ok = dict(allow_small_or_imprecise_dtypes=True)
                    pool.iota(iota_f[:, :], [[1, P]], base=0, channel_multiplier=0, **ok).then_inc(consts, 1)
                    pool.iota(pos[:, :, :], [[0, U], [1, P]], base=0, channel_multiplier=0, **ok).then_inc(consts, 1)
                    pool.iota(rbase[:, :, :], [[1, U], [0, P]], base=0, channel_multiplier=BLK, **ok)\
                        .then_inc(consts, 1)
                    pool.iota(e_idx[:, :, :], [[1, U], [U, NB]], base=0, channel_multiplier=0, **ok)\
                        .then_inc(consts, 1)
                    pool.iota(k_idx[:, :], [[1, U]], base=0, channel_multiplier=U, **ok).then_inc(consts, 1)

                ALL_CONSTS = 11

                @block.sync
                def _(sp):
                    sp.wait_ge(pads, 4)
                    for tile, array, off in row_loads:
                        left = E - whole - off
                        sp.dma_start(tile[0:E_FULL, :],
                                     array[off:off + whole].rearrange("(b i) -> b i", i=BLK)).then_inc(rows_in, 16)
                        sp.dma_start(tile[E_FULL:E_FULL + 1, 0:left],
                                     array[off + whole:off + whole + left].rearrange("(a i) -> a i", a=1))\
                            .then_inc(rows_in, 16)
                    sp.dma_start(w0[:, 0, :], Wl0).then_inc(w_in, 16)
                    sp.dma_start(w0[:, 1, :], Wr0).then_inc(w_in, 16)
                    sp.dma_start(w1[:, 0, :, :], Wl1.rearrange("(k p) n -> p k n", p=P)).then_inc(w_in, 16)
                    sp.dma_start(w1[:, 1, :, :], Wr1.rearrange("(k p) n -> p k n", p=P)).then_inc(w_in, 16)
                    sp.dma_start(w2[:, :, 0:D], Wl2.rearrange("(k p) n -> p k n", p=P)).then_inc(w_in, 16)
                    sp.dma_start(w2[:, :, D:2 * D], Wr2.rearrange("(k p) n -> p k n", p=P)).then_inc(w_in, 16)
                    for n, w in enumerate((Wd, Wc, Ws)):
                        sp.dma_start(w3[:, n * D:(n + 1) * D], w).then_inc(w_in, 16)
                    sp.dma_start(bias0_f[:, :], b0.rearrange("(a n) -> a n", a=1).to_broadcast([2, H])).then_inc(w_in, 16)
                    for n, b in enumerate((bd, bc, bs)):
                        sp.dma_start(bias3_f[:, n * D:(n + 1) * D],
                                     b.rearrange("(a n) -> a n", a=1).to_broadcast([2, D])).then_inc(w_in, 16)
                    sp.dma_start(b1_c[:, :], b1.rearrange("(k p) -> p k", p=P),
                                 allow_slow_non_contiguous=True).then_inc(w_in, 16)
                    for u in range(U):
                        sp.dma_start(b2_bc[:, u, :], b2.rearrange("(a n) -> a n", a=1).to_broadcast([P, D]))\
                            .then_inc(w_in, 16)
                    sp.wait_ge(consts, ALL_CONSTS)
                    sp.dma_start(pa_t[NP:NP + P, :], zeros[:, 0:D]).then_inc(filled, 16)
                    sp.dma_start(pb_t[NP:NP + P, :], zeros[:, :]).then_inc(filled, 16)
                    sp.dma_start(node_t.rearrange("(p k) v -> p (k v)", p=P),
                                 fill[:, :, :].rearrange("p k v -> p (k v)")).then_inc(filled, 16)
                    sp.wait_ge(filled, 48)

                N_W = 16 * (9 + 4 + 1 + U)

                @block.scalar
                def _(act):
                    act.wait_ge(w_in, N_W)
                    act.activation(W0h[:, :, :], w0[:, :, :], ACT.Copy).then_inc(w_hi, 1)
                    act.activation(W1h[:, :, :, :].rearrange("p a b c -> p (a b c)"),
                                   w1[:, :, :, :].rearrange("p a b c -> p (a b c)"), ACT.Copy).then_inc(w_hi, 1)
                    act.activation(W2h[:, :, :], w2[:, :, :], ACT.Copy).then_inc(w_hi, 1)
                    act.wait_ge(w3_turned, 1)
                    act.activation(W3h[:, :], bank[6][:, 0:3 * D], ACT.Copy).then_inc(w_hi, 1)

                arrays = [(slot, slot_T[:, :, :]), (src_f, src_T[:, :, :]), (srcy, srcy_T[:, :, :]),
                          (sidx, sidx_T[:, :, :]), (row, payload_T[:, :, :, 0]), (count, payload_T[:, :, :, 1])]

                @block.vector
                def _(dve):
                    done = [0]

                    def chain(ins):
                        done[0] += 1
                        ins.then_inc(step, 1)

                    def settle():
                        dve.wait_ge(step, done[0])

                    flat = "b u i -> b (u i)"
                    dve.wait_ge(rows_in, 16 * 8)
                    dve.wait_ge(consts, ALL_CONSTS)
                    for f, i in ((dst_f, dst_i), (next_f, next_i), (src_f, src_i), (typ_f, typ_i)):
                        chain(dve.tensor_copy(f[:, :, :].rearrange(flat), i[:, :]))
                    chain(dve.memset(same[:, :, :], 0.0))
                    settle()
                    chain(dve.tensor_tensor(same[:, :, 1:P], dst_f[:, :, 1:P], dst_f[:, :, 0:P - 1], ALU.is_equal))
                    for u in range(U):
                        chain(dve.tensor_scalar(diag[:, u, :], ident[0:NB, 0:NB], dst_f[:, u, 0:1], None, ALU.mult))
                    settle()
                    dve.tensor_copy(zp[:, :], ident[:, 0:1]).then_inc(diag_ready, 1)
                    chain(dve.tensor_scalar(starts[:, :, :], same[:, :, :], -1.0, 1.0, ALU.mult, ALU.add))
                    settle()
                    chain(dve.tensor_tensor(starts[:, :, :], starts[:, :, :], pos[:, :, :], ALU.mult))
                    settle()
                    chain(dve.tensor_tensor_scan(slot[:, :, :].rearrange(flat), same[:, :, :].rearrange(flat),
                                                 starts[:, :, :].rearrange(flat), 0.0, ALU.mult, ALU.add))
                    settle()
                    chain(dve.scalar_tensor_tensor(row[:, :, :], slot[:, :, :], float(U), rbase[:, :, :],
                                                   ALU.mult, ALU.add))
                    chain(dve.scalar_tensor_tensor(count[:, :, :], pos[:, :, :], 1.0, slot[:, :, :],
                                                   ALU.add, ALU.subtract))
                    chain(dve.tensor_scalar(first_run[:, :, :], slot[:, :, :], 0.0, None, ALU.is_equal))
                    chain(dve.tensor_scalar(last_count[:, :], slot[:, :, P - 1], -1.0, float(P), ALU.mult, ALU.add))
                    chain(dve.tensor_tensor(sidx[:, :, :], dst_f[:, :, :], next_f[:, :, :], ALU.is_equal))
                    chain(dve.tensor_scalar(typ_f[:, :, :], typ_f[:, :, :], 0.0, None, ALU.is_equal))
                    settle()
                    chain(dve.tensor_copy(tlast_i[:, :], row[:, :, P - 1]))
                    chain(dve.tensor_scalar(sidx[:, :, :], sidx[:, :, :], -1.0, 1.0, ALU.mult, ALU.add))
                    chain(dve.scalar_tensor_tensor(srcy[:, :, :], typ_f[:, :, :], -float(NP), src_f[:, :, :],
                                                   ALU.mult, ALU.add))
                    settle()
                    chain(dve.tensor_scalar(srcy[:, :, :], srcy[:, :, :], float(NP), None, ALU.add))
                    chain(dve.scalar_tensor_tensor(sidx[:, :, :], dst_f[:, :, :], -float(PAD_DST), sidx[:, :, :],
                                                   ALU.add, ALU.mult))
                    settle()
                    chain(dve.tensor_scalar(sidx[:, :, :], sidx[:, :, :], float(PAD_DST), None, ALU.add))
                    dve.wait_ge(bc_ready, 1)
                    bcast = bank[6][0:NB, 0:U * NB].rearrange("k (u b) -> k u b", u=U)
                    for u in range(U):
                        chain(dve.tensor_scalar(hit[:, :, :], bcast, dst_f[:, u, P - 1:P], None, ALU.is_equal))
                        settle()
                        chain(dve.scalar_tensor_tensor(M[:, u, :, :], e_idx[:, :, :], k_idx[:, u:u + 1],
                                                       hit[:, :, :], ALU.is_gt, ALU.mult))
                        settle()
                    dve.tensor_copy(zp[:, :], ident[:, 0:1]).then_inc(m_ready, 1)
                    dve.wait_ge(carry_ready, 1)
                    for u in range(U):
                        chain(dve.scalar_tensor_tensor(count[:, u, :], first_run[:, u, :], bank[7][0:NB, u:u + 1],
                                                       count[:, u, :], ALU.mult, ALU.add))
                    settle()
                    dve.tensor_copy(zp[:, :], ident[:, 0:1]).then_inc(arrays_ready, 1)
                    for n, (_, table) in enumerate(arrays):
                        dve.wait_ge(turned, n + 1)
                        chain(dve.tensor_copy(table.rearrange("p b u -> p u b"),
                                              bank[n][:, 0:U * NB].rearrange("p (u b) -> p u b", u=U)))
                    dve.wait_ge(w_hi, 4)
                    dve.tensor_tensor(W0l[:, :, :], w0[:, :, :], W0h[:, :, :].bitcast(F32), ALU.subtract)
                    dve.tensor_tensor(W1l[:, :, :, :].rearrange("p a b c -> p (a b c)"),
                                      w1[:, :, :, :].rearrange("p a b c -> p (a b c)"),
                                      W1h[:, :, :, :].rearrange("p a b c -> p (a b c)").bitcast(F32), ALU.subtract)
                    dve.tensor_tensor(W2l[:, :, :], w2[:, :, :], W2h[:, :, :].bitcast(F32), ALU.subtract)
                    chain(dve.tensor_copy(ones_r[:, :], ones[0:2, :]))
                    for f, h, l, b in ((bias0_f, bias0_h, bias0_l, bias0), (bias3_f, bias3_h, bias3_l, bias3)):
                        chain(dve.tensor_copy(h[:, :], f[:, :]))
                        settle()
                        chain(dve.tensor_tensor(l[:, :], f[:, :], h[:, :].bitcast(F32), ALU.subtract))
                        settle()
                        chain(dve.tensor_scalar(l[:, :], l[:, :], ident[0:2, 1:2], None, ALU.mult))
                        settle()
                        dve.scalar_tensor_tensor(b[:, :], h[:, :].bitcast(F32), ident[0:2, 0:1], l[:, :],
                                                 ALU.mult, ALU.add)
                    dve.tensor_tensor(W3l[:, :], bank[6][:, 0:3 * D], W3h[:, :].bitcast(F32), ALU.subtract)

                @block.tensor
                def _(pe):
                    pe.wait_ge(consts, ALL_CONSTS)
                    pe.wait_ge(diag_ready, 1)
                    for u in range(U):
                        mm = pe.matmul(bank[6][0:NB, u * NB:(u + 1) * NB], ones[0:NB, 0:NB], diag[:, u, :],
                                       start=True, stop=True)
                    mm.then_inc(bc_ready, 1)
                    pe.wait_ge(m_ready, 1)
                    for e in range(U):
                        for k in range(U):
                            mm = pe.matmul(bank[7][0:NB, e:e + 1], M[:, k, e, :], last_count[:, k:k + 1],
                                           start=(k == 0), stop=(k == U - 1))
                    mm.then_inc(carry_ready, 1)
                    pe.wait_ge(w_in, N_W)
                    for n in range(3):
                        mm = pe.transpose(bank[6][:, n * D:(n + 1) * D], w3[:, n * D:(n + 1) * D], ident[:, :])
                    mm.then_inc(w3_turned, 1)
                    pe.wait_ge(arrays_ready, 1)
                    for n, (array, _) in enumerate(arrays):
                        for u in range(U):
                            mm = pe.transpose(bank[n][:, u * NB:(u + 1) * NB], array[:, u, :], ident[0:NB, 0:NB])
                        mm.then_inc(turned, 1)

        def ln_stats(dve, rows, s, step, done):
            for u in range(U):
                dve.bn_stats(stats[:, s, u, :], rows[:, u, :]).then_inc(step, 1)
            dve.wait_ge(step, done + U)
            dve.nop(nofuse=True)
            for u in range(U):
                last = dve.bn_aggr(mv[:, s, u, :], stats[:, s, u, :])
            return last

        def ln_scalars(dve, s, b, std_ready, rstd_ready):
            dve.wait_ge(std_ready, b + 1)
            dve.reciprocal(rstd[:, s, :], std[:, s, :]).then_inc(rstd_ready, 1)
            dve.wait_ge(rstd_ready, 2 * b + 1)
            dve.scalar_tensor_tensor(nbias[:, s, :], mv[:, s, :, 0], -1.0, rstd[:, s, :],
                                     ALU.mult, ALU.mult).then_inc(rstd_ready, 1)

        def layer_norm_x():
            x_in = [sem(f"ln_x_in{s}") for s in range(R)]
            stored = [sem(f"ln_stored{s}") for s in range(2)]
            step = sem("ln_step")
            mean_var = sem("ln_mean_var")
            std_ready = sem("ln_std")
            rstd_ready = sem("ln_rstd")
            h_ready = sem("ln_h")
            staged = sem("ln_staged")
            scattered = [sem(f"ln_scattered{s}") for s in range(R)]
            with nc.Block() as block:

                @block.sync
                def _(sp):
                    def load(b, s, i):
                        wait(sp, h_ready, b - R + 1)
                        load_x(sp, own, b, s, 0, x_in[s])

                    lagged(sp, load)

                @block.vector
                def _(dve):
                    def statistics(b, s, i):
                        dve.wait_ge(x_in[s], 16 * (i + 1))
                        wait(dve, h_ready, b - R + 1)
                        rows = own[:, s, 0:U * D].rearrange("p (u d) -> p u d", u=U)
                        ln_stats(dve, rows, s, step, U * b).then_inc(mean_var, 1)

                    def scalars(b, s, i):
                        ln_scalars(dve, s, b, std_ready, rstd_ready)

                    lagged(dve, statistics, scalars)

                @block.scalar
                def _(act):
                    def deviation(b, s, i):
                        act.wait_ge(mean_var, b + 1)
                        act.activation(std[:, s, :], mv[:, s, :, 1], ACT.Sqrt, bias=eps_c[:, 0:1])\
                            .then_inc(std_ready, 1)

                    def apply(b, s, i):
                        act.wait_ge(rstd_ready, 2 * b + 2)
                        wait(act, stored[s % 2], 16 * uses(s, i))
                        for u in range(U):
                            last = act.activation(res[:, s % 2, u * D:(u + 1) * D], own[:, s, u * D:(u + 1) * D],
                                                  ACT.Relu, bias=nbias[:, s, u:u + 1], scale=rstd[:, s, u:u + 1])
                        last.then_inc(h_ready, 1)

                    def store(b, s, i):
                        act.wait_ge(h_ready, b + 1)
                        act.dma_start(rows_of(h0_t, b), res[:, s % 2, 0:U * D]).then_inc(stored[s % 2], 16)

                    lagged(act, deviation, apply, store)
                    for s in range(2):
                        act.wait_ge(stored[s], 16 * NB // 2)

                @block.gpsimd
                def _(pool):
                    def scatter(b, s, i):
                        wait(pool, scattered[s], 16 * U * i)
                        pool.tensor_copy(stage[:, s, :], sidx_T[:, at(b), :].rearrange("p a u -> p (a u)"))\
                            .then_inc(staged, 1)
                        pool.tensor_copy(pay_stage[:, s, :], payload_T[:, at(b), :, :].rearrange(
                            "p a u v -> p (a u v)")).then_inc(staged, 1)
                        pool.wait_ge(staged, 2 * b + 2)
                        pool.nop(nofuse=True)
                        for u in range(U):
                            pool.indirect_dma_start(
                                node_t, bass.IndirectOffsetOnAxis(stage[:, s, u:u + 1], 0),
                                pay_stage[:, s, 2 * u:2 * u + 2], None,
                                bounds_check=NP - 1, oob_is_err=False).then_inc(scattered[s], 16)

                    lagged(pool, scatter)
                    for s in range(R):
                        pool.wait_ge(scattered[s], 16 * U * NI)

        def load_node_entries():
            entries = sb("entries", [P, NB, U, 2])
            loaded = sem("ne_loaded")
            split = sem("ne_split")
            with nc.Block() as block:

                @block.sync
                def _(sp):
                    sp.dma_start(entries[:, :, :, :].rearrange("p b u v -> p b (u v)"),
                                 node_t.rearrange("(b p u) v -> p b (u v)", p=P, u=U)).then_inc(loaded, 16)

                @block.vector
                def _(dve):
                    dve.wait_ge(loaded, 16)
                    dve.tensor_copy(node_row[:, :, :], entries[:, :, :, 0]).then_inc(split, 1)
                    dve.reciprocal(node_inv[:, :, :], entries[:, :, :, 1]).then_inc(split, 1)

        def gather_blocks(pool, table, index, width, nth, freed):
            def gather(b, s, i):
                if s % 2 == 0:
                    wait(pool, gathered[s], gathers(nth, i))
                    wait(pool, gathered[s + 1], gathers(nth, i))
                    pool.tensor_copy(stage[:, s:s + 2, :], index[:, bass.ds(b, 2), :]).then_inc(staged, 1)
                wait(pool, freed, b - R + 1)
                pool.wait_ge(staged, 2 * (NI * nth + i) + s // 2 + 1)
                pool.nop(nofuse=True)
                for u in range(U):
                    pool.indirect_dma_start(raw[:, s, u * width:(u + 1) * width], None, table,
                                            bass.IndirectOffsetOnAxis(stage[:, s, u:u + 1], 0))\
                        .then_inc(gathered[s], 16)

            lagged(pool, gather)

        def run_sums(tag, nth, width, table, index, p_t):
            n_banks = width * U // 512
            hi = sem(tag + "_hi")
            lo = sem(tag + "_lo")
            onehot = sem(tag + "_onehot")
            summed = sem(tag + "_summed")
            out_a = sem(tag + "_out_a")
            out_v = sem(tag + "_out_v")
            stored = [sem(f"{tag}_stored{s}") for s in range(2)]
            size = U * width
            with nc.Block() as block:

                @block.gpsimd
                def _(pool):
                    gather_blocks(pool, table, index, width, nth, lo)

                @block.scalar
                def _(act):
                    def upper(b, s, i):
                        act.wait_ge(gathered[s], gathers(nth, i + 1))
                        wait(act, summed, b - 1)
                        act.activation(big_h[:, s % 2, 0:size], raw[:, s, 0:size], ACT.Copy).then_inc(hi, 1)

                    def evacuate(b, s, i):
                        act.wait_ge(summed, b + 1)
                        wait(act, stored[s % 2], 16 * uses(s, i))
                        act.activation(res[:, s % 2, 0:512], bank[s * n_banks][:, :], ACT.Copy).then_inc(out_a, 1)

                    lagged(act, upper, evacuate)

                @block.vector
                def _(dve):
                    def split(b, s, i):
                        wait(dve, summed, b - 1)
                        for u in range(U):
                            last = dve.tensor_scalar(S[:, s % 2, u, :], iota_f[:, :],
                                                     slot_T[:, at(b), u:u + 1].rearrange("p a u -> p (a u)"),
                                                     None, ALU.is_equal)
                        last.then_inc(onehot, 1)
                        dve.wait_ge(gathered[s], gathers(nth, i + 1))
                        dve.wait_ge(hi, b + 1)
                        dve.tensor_tensor(big_l[:, s % 2, 0:size], raw[:, s, 0:size],
                                          big_h[:, s % 2, 0:size].bitcast(F32), ALU.subtract).then_inc(lo, 1)

                    def evacuate(b, s, i):
                        dve.wait_ge(summed, b + 1)
                        wait(dve, stored[s % 2], 16 * uses(s, i))
                        dve.tensor_copy(res[:, s % 2, 512:1024], bank[2 * s + 1][:, :]).then_inc(out_v, 1)

                    lagged(dve, split, *([evacuate] if n_banks == 2 else []))

                @block.tensor
                def _(pe):
                    def add_up(b, s, i):
                        pe.wait_ge(onehot, b + 1)
                        pe.wait_ge(lo, b + 1)
                        wait(pe, out_a, b - R + 1)
                        if n_banks == 2:
                            wait(pe, out_v, b - R + 1)
                        for u in range(U):
                            c = u * width
                            o = bank[s * n_banks + c // 512][:, c % 512:c % 512 + width]
                            mm = accumulate(pe, o, [(S[:, s % 2, u, :], big_h[:, s % 2, c:c + width]),
                                                    (S[:, s % 2, u, :], big_l[:, s % 2, c:c + width])])
                        mm.then_inc(summed, 1)

                    lagged(pe, add_up)

                @block.sync
                def _(sp):
                    def store(b, s, i):
                        sp.wait_ge(out_a, b + 1)
                        if n_banks == 2:
                            sp.wait_ge(out_v, b + 1)
                        sp.dma_start(rows_of(p_t, b), res[:, s % 2, 0:size]).then_inc(stored[s % 2], 16)

                    lagged(sp, store)
                    for s in range(2):
                        sp.wait_ge(stored[s], 16 * NB // 2)

        def carry_runs(tag, width, p_t):
            gathered = sem(tag + "_c_gathered")
            loaded = sem(tag + "_c_loaded")
            carried = sem(tag + "_c_carried")
            added = sem(tag + "_c_added")
            stored = sem(tag + "_c_stored")
            firsts = p_t[0:NP, :].rearrange("(b q) d -> b (q d)", q=BLK)[:, 0:U * width]
            n_banks = width * U // 512
            with nc.Block() as block:

                @block.gpsimd
                def _(pool):
                    for u in range(U):
                        pool.indirect_dma_start(raw[0:NB, 0, u * width:(u + 1) * width], None, p_t,
                                                bass.IndirectOffsetOnAxis(tlast_i[:, u:u + 1], 0))\
                            .then_inc(gathered, 16)

                @block.sync
                def _(sp):
                    sp.dma_start(own[0:NB, 0, 0:U * width], firsts).then_inc(loaded, 16)
                    sp.wait_ge(added, n_banks)
                    sp.dma_start(firsts, res[0:NB, 0, 0:U * width]).then_inc(stored, 16)
                    sp.wait_ge(stored, 16)

                @block.tensor
                def _(pe):
                    pe.wait_ge(gathered, 16 * U)
                    for e in range(U):
                        c = e * width
                        for k in range(U):
                            mm = pe.matmul(bank[c // 512][0:NB, c % 512:c % 512 + width], M[:, k, e, :],
                                           raw[0:NB, 0, k * width:(k + 1) * width],
                                           start=(k == 0), stop=(k == U - 1))
                    mm.then_inc(carried, 1)

                @block.vector
                def _(dve):
                    dve.wait_ge(loaded, 16)
                    dve.wait_ge(carried, 1)
                    for n in range(n_banks):
                        dve.tensor_tensor(res[0:NB, 0, n * 512:(n + 1) * 512], own[0:NB, 0, n * 512:(n + 1) * 512],
                                          bank[n][0:NB, :], ALU.add).then_inc(added, 1)

        def mean_rows(dve, b, s, width, nth, i, scaled):
            dve.wait_ge(gathered[s], gathers(nth, i + 1))
            for u in range(U):
                c = slice(u * width, (u + 1) * width)
                last = dve.tensor_scalar(raw[:, s, c], raw[:, s, c],
                                         node_inv[:, at(b), u:u + 1].rearrange("p a u -> p (a u)"), None, ALU.mult)
            last.then_inc(scaled, 1)

        def sage_0(nth):
            own_in = [sem(f"b0_own_in{s}") for s in range(R)]
            stored = [sem(f"b0_stored{s}") for s in range(2)]
            scaled = sem("b0_scaled")
            turned = sem("b0_turned")
            hi = sem("b0_hi")
            lo = sem("b0_lo")
            dense = sem("b0_dense")
            h_ready = sem("b0_h")
            with nc.Block() as block:

                @block.gpsimd
                def _(pool):
                    gather_blocks(pool, pa_t, node_row, D, nth, turned)

                @block.sync
                def _(sp):
                    def load(b, s, i):
                        wait(sp, turned, b - R + 1)
                        sp.dma_start(own[:, s, 0:U * D], rows_of(h0_t, b)).then_inc(own_in[s], 16)

                    lagged(sp, load)

                @block.vector
                def _(dve):
                    def scale(b, s, i):
                        mean_rows(dve, b, s, D, nth, i, scaled)

                    def lower(b, s, i):
                        dve.wait_ge(hi, b + 1)
                        wait(dve, dense, b - 1)
                        q = s % 2
                        dve.tensor_tensor(big_l[:, q, 0:512], bank[2 * q][:, :], big_h[:, q, 0:512].bitcast(F32),
                                          ALU.subtract)
                        dve.tensor_tensor(own_l[:, q, 0:512], bank[2 * q + 1][:, :],
                                          own_h[:, q, 0:512].bitcast(F32), ALU.subtract).then_inc(lo, 1)

                    lagged(dve, scale, lower)

                @block.scalar
                def _(act):
                    def upper(b, s, i):
                        act.wait_ge(turned, b + 1)
                        wait(act, dense, b - 1)
                        q = s % 2
                        act.activation(big_h[:, q, 0:512], bank[2 * q][:, :], ACT.Copy)
                        act.activation(own_h[:, q, 0:512], bank[2 * q + 1][:, :], ACT.Copy).then_inc(hi, 1)

                    def relu(b, s, i):
                        q = s % 2
                        act.wait_ge(dense, b + 1)
                        wait(act, stored[q], 16 * uses(s, i))
                        for n in range(2):
                            last = act.activation(res[:, q, n * 512:(n + 1) * 512], bank[4 + 2 * q + n][:, :],
                                                  ACT.Relu)
                        last.then_inc(h_ready, 1)

                    def store(b, s, i):
                        act.wait_ge(h_ready, b + 1)
                        act.dma_start(rows_of(h1_t, b), res[:, s % 2, :]).then_inc(stored[s % 2], 16)

                    lagged(act, None, upper, relu, store)
                    for s in range(2):
                        act.wait_ge(stored[s], 16 * NB // 2)

                @block.tensor
                def _(pe):
                    def turn(b, s, i):
                        pe.wait_ge(scaled, b + 1)
                        pe.wait_ge(own_in[s], 16 * (i + 1))
                        wait(pe, lo, b - 1)
                        for n, rows in enumerate((raw, own)):
                            for u in range(U):
                                mm = pe.transpose(bank[2 * (s % 2) + n][:, u * P:(u + 1) * P],
                                                  rows[:, s, u * D:(u + 1) * D], ident[:, :])
                        mm.then_inc(turned, 1)

                    def product(b, s, i):
                        pe.wait_ge(lo, b + 1)
                        wait(pe, h_ready, b - 1)
                        q = s % 2
                        for u in range(U):
                            c = slice(u * P, (u + 1) * P)
                            mm = accumulate(pe, bank[4 + 2 * q + u // 2][:, (u % 2) * H:(u % 2 + 1) * H], [
                                (ones_r[:, :], bias0[:, :]),
                                (big_h[:, q, c], W0h[:, 0, :]), (big_h[:, q, c], W0l[:, 0, :]),
                                (big_l[:, q, c], W0h[:, 0, :]), (own_h[:, q, c], W0h[:, 1, :]),
                                (own_h[:, q, c], W0l[:, 1, :]), (own_l[:, q, c], W0h[:, 1, :])])
                        mm.then_inc(dense, 1)

                    lagged(pe, None, turn, product)

        def sage_1(nth):
            own_in = [sem(f"b1_own_in{s}") for s in range(R)]
            x_in = [sem(f"b1_x_in{s}") for s in range(R)]
            stored = [sem(f"b1_stored{s}") for s in range(2)]
            scaled = sem("b1_scaled")
            turned = sem("b1_turned")
            hi = sem("b1_hi")
            lo = sem("b1_lo")
            dense = sem("b1_dense")
            relu_done = sem("b1_relu")
            h2_hi = sem("b1_h2_hi")
            h2_lo = sem("b1_h2_lo")
            dense2 = sem("b1_dense2")
            g_out = sem("b1_g_out")
            xb = sem("b1_xb")
            s_out = sem("b1_s_out")
            g_half = res2[:, :, 0:U * D]
            s_half = res2[:, :, U * D:2 * U * D]
            with nc.Block() as block:

                @block.gpsimd
                def _(pool):
                    gather_blocks(pool, pb_t, node_row, H, nth, turned)

                @block.sync
                def _(sp):
                    def load(b, s, i):
                        wait(sp, turned, b - R + 1)
                        sp.dma_start(own[:, s, :], rows_of(h1_t, b)).then_inc(own_in[s], 16)

                    def load_residual(b, s, i):
                        wait(sp, s_out, b - R + 1)
                        load_x(sp, x1_b, b, s, 0, x_in[s])

                    lagged(sp, load, load_residual)

                @block.vector
                def _(dve):
                    def scale(b, s, i):
                        mean_rows(dve, b, s, H, nth, i, scaled)

                    def lower(b, s, i):
                        wait(dve, dense, b - 1)
                        for n in range(4):
                            dve.wait_ge(hi, 4 * b + n + 1)
                            h, l = (big_h, big_l) if n < 2 else (own_h, own_l)
                            c = slice((n % 2) * 512, (n % 2 + 1) * 512)
                            dve.tensor_tensor(l[:, s % 2, c], bank[n][:, :], h[:, s % 2, c].bitcast(F32),
                                              ALU.subtract).then_inc(lo, 1)

                    def split_h2(b, s, i):
                        q = s % 2
                        dve.wait_ge(relu_done, b + 1)
                        wait(dve, dense2, b - 1)
                        dve.tensor_copy(h2_h[:, q, :], res[:, q, :]).then_inc(h2_hi, 1)
                        dve.wait_ge(h2_hi, b + 1)
                        dve.tensor_tensor(h2_l[:, q, :], res[:, q, :], h2_h[:, q, :].bitcast(F32), ALU.subtract)\
                            .then_inc(h2_lo, 1)

                    def residual(b, s, i):
                        q = s % 2
                        dve.wait_ge(x_in[s], 16 * (i + 1))
                        dve.tensor_tensor(x1_b[:, s, :], x1_b[:, s, :], b2_bc[:, :, :].rearrange("p u d -> p (u d)"),
                                          ALU.add).then_inc(xb, 1)
                        dve.wait_ge(g_out, b + 1)
                        dve.wait_ge(xb, b + 1)
                        wait(dve, stored[q], 32 * uses(s, i))
                        for n in range(2):
                            c = slice(n * 2 * D, (n + 1) * 2 * D)
                            last = dve.tensor_tensor(
                                s_half[:, q, c].rearrange("p (u d) -> p u d", u=2),
                                bank[6 + n][:, :].rearrange("p (u g d) -> p u g d", u=2, g=2)[:, :, 1, :],
                                x1_b[:, s, c].rearrange("p (u d) -> p u d", u=2), ALU.add)
                        last.then_inc(s_out, 1)

                    lagged(dve, scale, lower, split_h2, residual)

                @block.scalar
                def _(act):
                    def upper(b, s, i):
                        wait(act, dense, b - 1)
                        act.wait_ge(turned, b + 1)
                        for n in range(4):
                            h = big_h if n < 2 else own_h
                            act.activation(h[:, s % 2, (n % 2) * 512:(n % 2 + 1) * 512], bank[n][:, :], ACT.Copy)\
                                .then_inc(hi, 1)

                    def relu(b, s, i):
                        act.wait_ge(dense, b + 1)
                        wait(act, h2_lo, b - 1)
                        for m in range(K):
                            last = act.activation(res[:, s % 2, m * 512:(m + 1) * 512], bank[4 + m][:, :],
                                                  ACT.Relu, bias=b1_c[:, m:m + 1])
                        last.then_inc(relu_done, 1)

                    def evacuate(b, s, i):
                        q = s % 2
                        act.wait_ge(dense2, b + 1)
                        wait(act, stored[q], 32 * uses(s, i))
                        for n in range(2):
                            last = act.activation(
                                g_half[:, q, n * 2 * D:(n + 1) * 2 * D].rearrange("p (u d) -> p u d", u=2),
                                bank[6 + n][:, :].rearrange("p (u g d) -> p u g d", u=2, g=2)[:, :, 0, :], ACT.Copy)
                        last.then_inc(g_out, 1)

                    def store(b, s, i):
                        act.wait_ge(g_out, b + 1)
                        act.dma_start(rows_of(g2_t, b), g_half[:, s % 2, :]).then_inc(stored[s % 2], 16)
                        act.wait_ge(s_out, b + 1)
                        act.dma_start(rows_of(s2_t, b), s_half[:, s % 2, :]).then_inc(stored[s % 2], 16)

                    lagged(act, None, upper, relu, evacuate, store)
                    for s in range(2):
                        act.wait_ge(stored[s], 32 * NB // 2)

                @block.tensor
                def _(pe):
                    def turn(b, s, i):
                        pe.wait_ge(scaled, b + 1)
                        pe.wait_ge(own_in[s], 16 * (i + 1))
                        wait(pe, lo, 4 * b)
                        for n in range(4):
                            rows = raw if n < 2 else own
                            for u in range(U):
                                c = u * H + (n % 2) * P
                                mm = pe.transpose(bank[n][:, u * P:(u + 1) * P], rows[:, s, c:c + P], ident[:, :])
                        mm.then_inc(turned, 1)

                    def product(b, s, i):
                        q = s % 2
                        pe.wait_ge(lo, 4 * b + 4)
                        wait(pe, relu_done, b)
                        for m in range(K):
                            products = []
                            for w, (h, l) in enumerate(((big_h, big_l), (own_h, own_l))):
                                for k in range(K):
                                    wh = W1h[:, w, k, m * P:(m + 1) * P]
                                    wl = W1l[:, w, k, m * P:(m + 1) * P]
                                    c = slice(k * 512, (k + 1) * 512)
                                    products += [(wh, h[:, q, c]), (wh, l[:, q, c]), (wl, h[:, q, c])]
                            mm = accumulate(pe, bank[4 + m][:, :], products)
                        mm.then_inc(dense, 1)

                    def product_2(b, s, i):
                        q = s % 2
                        pe.wait_ge(h2_lo, b + 1)
                        wait(pe, s_out, b)
                        for u in range(U):
                            products = []
                            for k in range(K):
                                c = slice(k * 512 + u * P, k * 512 + (u + 1) * P)
                                products += [(h2_h[:, q, c], W2h[:, k, :]), (h2_h[:, q, c], W2l[:, k, :]),
                                             (h2_l[:, q, c], W2h[:, k, :])]
                            mm = accumulate(pe, bank[6 + u // 2][:, (u % 2) * 2 * D:(u % 2 + 1) * 2 * D], products)
                        mm.then_inc(dense2, 1)

                    lagged(pe, None, turn, product, product_2)

        def sage_2(nth):
            s_in = [sem(f"b2_s_in{s}") for s in range(R)]
            stored = [sem(f"b2_stored{s}") for s in range(2)]
            x_stored = [sem(f"b2_x_stored{s}") for s in range(R)]
            step = sem("b2_step")
            x1_ready = sem("b2_x1")
            mean_var = sem("b2_mean_var")
            std_ready = sem("b2_std")
            rstd_ready = sem("b2_rstd")
            h_ready = sem("b2_h")
            turned = sem("b2_turned")
            hi = sem("b2_hi")
            lo = sem("b2_lo")
            dense = sem("b2_dense")
            y_act = sem("b2_y_act")
            y_dve = sem("b2_y_dve")
            with nc.Block() as block:

                @block.gpsimd
                def _(pool):
                    gather_blocks(pool, pa_t, node_row, D, nth, x1_ready)

                @block.sync
                def _(sp):
                    def load(b, s, i):
                        wait(sp, x1_ready, b - R + 1)
                        sp.dma_start(own[:, s, 0:U * D], rows_of(s2_t, b)).then_inc(s_in[s], 16)

                    def store_x1(b, s, i):
                        sp.wait_ge(x1_ready, b + 1)
                        sp.dma_start(rows_of(x1_t, b), x1_b[:, s, :]).then_inc(x_stored[s], 16)

                    lagged(sp, load, None, store_x1)
                    for s in range(R):
                        sp.wait_ge(x_stored[s], 16 * NI)

                @block.vector
                def _(dve):
                    def residual(b, s, i):
                        dve.wait_ge(s_in[s], 16 * (i + 1))
                        dve.wait_ge(gathered[s], gathers(nth, i + 1))
                        wait(dve, x_stored[s], 16 * i)
                        wait(dve, h_ready, b - R + 1)
                        for u in range(U):
                            c = slice(u * D, (u + 1) * D)
                            last = dve.scalar_tensor_tensor(
                                x1_b[:, s, c], raw[:, s, c], node_inv[:, at(b), u:u + 1].rearrange("p a u -> p (a u)"),
                                own[:, s, c], ALU.mult, ALU.add)
                        last.then_inc(x1_ready, 1)
                        dve.wait_ge(x1_ready, b + 1)
                        rows = x1_b[:, s, :].rearrange("p (u d) -> p u d", u=U)
                        ln_stats(dve, rows, s, step, U * b).then_inc(mean_var, 1)

                    def scalars(b, s, i):
                        ln_scalars(dve, s, b, std_ready, rstd_ready)

                    def lower(b, s, i):
                        q = s % 2
                        dve.wait_ge(hi, b + 1)
                        wait(dve, dense, b - 1)
                        dve.tensor_tensor(big_l[:, q, 0:512], bank[q][:, :], big_h[:, q, 0:512].bitcast(F32),
                                          ALU.subtract).then_inc(lo, 1)

                    def evacuate(b, s, i):
                        q = s % 2
                        dve.wait_ge(dense, b + 1)
                        wait(dve, stored[q], 48 * uses(s, i))
                        y = res2[:, q, :].rearrange("p (n u d) -> p n u d", n=3, u=U)
                        for u in range(2, U):
                            last = dve.tensor_copy(y[:, :, u, :],
                                                   bank[2 + u][:, 0:3 * D].rearrange("p (n d) -> p n d", n=3))
                        last.then_inc(y_dve, 1)

                    lagged(dve, residual, scalars, lower, evacuate)

                @block.scalar
                def _(act):
                    def deviation(b, s, i):
                        act.wait_ge(mean_var, b + 1)
                        act.activation(std[:, s, :], mv[:, s, :, 1], ACT.Sqrt, bias=eps_c[:, 0:1])\
                            .then_inc(std_ready, 1)

                    def apply(b, s, i):
                        act.wait_ge(rstd_ready, 2 * b + 2)
                        wait(act, turned, b - 1)
                        for u in range(U):
                            last = act.activation(h3_b[:, s % 2, u * D:(u + 1) * D], x1_b[:, s, u * D:(u + 1) * D],
                                                  ACT.Relu, bias=nbias[:, s, u:u + 1], scale=rstd[:, s, u:u + 1])
                        last.then_inc(h_ready, 1)

                    def upper(b, s, i):
                        act.wait_ge(turned, b + 1)
                        wait(act, dense, b - 1)
                        act.activation(big_h[:, s % 2, 0:512], bank[s % 2][:, :], ACT.Copy).then_inc(hi, 1)

                    def evacuate(b, s, i):
                        q = s % 2
                        act.wait_ge(dense, b + 1)
                        wait(act, stored[q], 48 * uses(s, i))
                        y = res2[:, q, :].rearrange("p (n u d) -> p n u d", n=3, u=U)
                        for u in range(2):
                            last = act.activation(y[:, :, u, :],
                                                  bank[2 + u][:, 0:3 * D].rearrange("p (n d) -> p n d", n=3), ACT.Copy)
                        last.then_inc(y_act, 1)

                    def store(b, s, i):
                        act.wait_ge(y_act, b + 1)
                        act.wait_ge(y_dve, b + 1)
                        for n, t in enumerate((y_t[0:NP, :], y_t[NP:2 * NP, :], self_t)):
                            act.dma_start(rows_of(t, b), res2[:, s % 2, n * U * D:(n + 1) * U * D])\
                                .then_inc(stored[s % 2], 16)

                    lagged(act, deviation, apply, upper, evacuate, store)
                    for s in range(2):
                        act.wait_ge(stored[s], 48 * NB // 2)

                @block.tensor
                def _(pe):
                    def turn(b, s, i):
                        pe.wait_ge(h_ready, b + 1)
                        wait(pe, lo, b - 1)
                        for u in range(U):
                            mm = pe.transpose(bank[s % 2][:, u * P:(u + 1) * P], h3_b[:, s % 2, u * D:(u + 1) * D],
                                              ident[:, :])
                        mm.then_inc(turned, 1)

                    def product(b, s, i):
                        q = s % 2
                        pe.wait_ge(lo, b + 1)
                        wait(pe, y_act, b)
                        wait(pe, y_dve, b)
                        for u in range(U):
                            c = slice(u * P, (u + 1) * P)
                            mm = accumulate(pe, bank[2 + u][:, 0:3 * D], [
                                (ones_r[:, :], bias3[:, :]),
                                (big_h[:, q, c], W3h[:, :]), (big_h[:, q, c], W3l[:, :]),
                                (big_l[:, q, c], W3h[:, :])])
                        mm.then_inc(dense, 1)

                    lagged(pe, turn, product)

        def relational(nth):
            x_in = [sem(f"b3_x_in{s}") for s in range(R)]
            stored = [sem(f"b3_stored{s}") for s in range(2)]
            added = sem("b3_added")
            relu_done = sem("b3_relu")
            o_ready = sem("b3_out")
            with nc.Block() as block:

                @block.gpsimd
                def _(pool):
                    gather_blocks(pool, pa_t, node_row, D, nth, added)

                @block.sync
                def _(sp):
                    def load(b, s, i):
                        wait(sp, o_ready, b - R + 1)
                        sp.dma_start(own[:, s, 0:U * D], rows_of(self_t, b)).then_inc(x_in[s], 16)
                        sp.dma_start(own[:, s, U * D:2 * U * D], rows_of(x1_t, b)).then_inc(x_in[s], 16)

                    lagged(sp, load)

                @block.vector
                def _(dve):
                    def add_self(b, s, i):
                        dve.wait_ge(x_in[s], 32 * (i + 1))
                        dve.wait_ge(gathered[s], gathers(nth, i + 1))
                        wait(dve, relu_done, b - 1)
                        dve.tensor_tensor(res2[:, s % 2, 0:U * D], raw[:, s, 0:U * D], own[:, s, 0:U * D], ALU.add)\
                            .then_inc(added, 1)

                    def residual(b, s, i):
                        q = s % 2
                        dve.wait_ge(relu_done, b + 1)
                        if not isinstance(b, int) or b - 2 <= FULL:
                            wait(dve, stored[q], 16 * uses(s, i))
                        dve.tensor_tensor(res[:, q, U * D:2 * U * D], res[:, q, 0:U * D], own[:, s, U * D:2 * U * D],
                                          ALU.add).then_inc(o_ready, 1)

                    lagged(dve, add_self, residual)

                @block.scalar
                def _(act):
                    def relu(b, s, i):
                        act.wait_ge(added, b + 1)
                        wait(act, o_ready, b - 1)
                        act.activation(res[:, s % 2, 0:U * D], res2[:, s % 2, 0:U * D], ACT.Relu).then_inc(relu_done, 1)

                    def store(b, s, i):
                        act.wait_ge(o_ready, b + 1)
                        q = s % 2
                        if isinstance(b, int) and b > FULL:
                            return
                        if isinstance(b, int) and b == FULL:
                            act.dma_start(out[b * BLK:N, :].rearrange("(p u) d -> p (u d)", u=U),
                                          res[0:TAIL, q, U * D:2 * U * D]).then_inc(stored[q], 16)
                        else:
                            act.dma_start(rows_of(out, b), res[:, q, U * D:2 * U * D]).then_inc(stored[q], 16)

                    lagged(act, relu, None, store)
                    for s in range(2):
                        act.wait_ge(stored[s], 16 * len(range(s, FULL + 1, 2)))

        with ExitStack() as scratch:
            run(prepare, scratch)

        stage = sb("stage", [P, R, U], I32)
        raw = sb("raw", [P, R, U * H])
        own = sb("own", [P, R, U * H])
        big_h = sb("big_h", [P, 2, U * H], F32R)
        big_l = sb("big_l", [P, 2, U * H], F32R)
        own_h = sb("own_h", [P, 2, U * H], F32R)
        own_l = sb("own_l", [P, 2, U * H], F32R)
        S = sb("S", [P, 2, U, P], F32R)
        res = sb("res", [P, 2, U * H])
        res2 = sb("res2", [P, 2, U * 3 * D])
        x1_b = sb("x1_b", [P, R, U * D])
        h3_b = sb("h3_b", [P, 2, U * D])
        stats = sb("stats", [P, R, U, 6])
        mv = sb("mv", [P, R, U, 2])
        std = sb("std", [P, R, U])
        rstd = sb("rstd", [P, R, U])
        nbias = sb("nbias", [P, R, U])
        pay_stage = sb("pay_stage", [P, R, 2 * U])
        h2_h = sb("h2_h", [P, 2, U * H], F32R)
        h2_l = sb("h2_l", [P, 2, U * H], F32R)

        run(layer_norm_x)
        run(load_node_entries)
        run(run_sums, "a0", 0, D, h0_t, src_T, pa_t)
        run(carry_runs, "a0", D, pa_t)
        run(sage_0, 1)
        run(run_sums, "a1", 2, H, h1_t, src_T, pb_t)
        run(carry_runs, "a1", H, pb_t)
        run(sage_1, 3)
        run(run_sums, "a2", 4, D, g2_t, src_T, pa_t)
        run(carry_runs, "a2", D, pa_t)
        run(sage_2, 5)
        run(run_sums, "a3", 6, D, y_t, srcy_T, pa_t)
        run(carry_runs, "a3", D, pa_t)
        run(relational, 7)


INPUTS = ["x", "src", "dst", "edge_type_2", "L0_gnn_Wl0", "L0_gnn_b0", "L0_gnn_Wr0", "L0_gnn_Wl1", "L0_gnn_b1",
          "L0_gnn_Wr1", "L0_gnn_Wl2", "L0_gnn_b2", "L0_gnn_Wr2", "L1_gnn_W_data", "L1_gnn_b_data",
          "L1_gnn_W_control", "L1_gnn_b_control", "L1_gnn_W_self", "L1_gnn_b_self"]


def kernel(**inputs):
    import numpy as np
    import concourse.bacc as bacc
    from concourse.bass_utils import run_bass_kernel_spmd

    nc = bacc.Bacc("TRN2", target_bir_lowering=False, num_devices=1)
    arrays, args = {}, []
    for name in INPUTS:
        a = np.ascontiguousarray(inputs[name])
        arrays["in_" + name] = a
        args.append(nc.dram_tensor("in_" + name, a.shape, mybir.dt.from_np(a.dtype), kind="ExternalInput").ap())
    out = nc.dram_tensor("out", inputs["x"].shape, F32, kind="ExternalOutput").ap()
    build(nc, *args, out)
    return run_bass_kernel_spmd(nc, [arrays], core_ids=[0]).results[0]["out"]
```

```python
from contextlib import ExitStack

import concourse.bass as bass
from concourse import mybir

ALU = mybir.AluOpType
ACT = mybir.ActivationFunctionType
F32 = mybir.dt.float32
F32R = mybir.dt.float32r
I32 = mybir.dt.int32

P = 128
U = 4
BLK = P * U
R = 4
EPS = 1e-5
PAD_DST = 1 << 20


def peeled_loop(eng, n, body):
    body(0)
    body(1)
    with eng.Fori(2, n - 1) as i:
        body(i)
    body(n - 1)


def wait(eng, sem, value):
    if isinstance(value, int) and value <= 0:
        return
    eng.wait_ge(sem, value)


def build(nc, x, src, dst, etype, Wl0, b0, Wr0, Wl1, b1, Wr1, Wl2, b2, Wr2,
          Wd, bd, Wc, bc, Ws, bs, out):
    N, D = x.shape
    E = src.shape[0]
    H = Wl0.shape[1]
    K = H // P
    NB = -(-max(N, E) // (2 * BLK)) * 2
    NI = -(-NB // R)
    NP = NB * BLK
    FULL = N // BLK
    TAIL = (N - FULL * BLK) // U
    E_FULL = E // BLK
    assert D == P and H == 2 * P and TAIL * U == N - FULL * BLK
    assert (NI - 1) * R <= FULL == NB - 1
    ZROW = NP

    def dram(name, shape, dt=F32):
        return nc.dram_tensor(name, shape, dt, kind="Internal").ap()

    h0_t = dram("h0_t", (NP, D))
    h1_t = dram("h1_t", (NP, H))
    h2_t = dram("h2_t", (NP, H))
    s2_t = dram("s2_t", (NP, D))
    xb_t = dram("xb_t", (NP, D))
    x1_t = dram("x1_t", (NP, D))
    self_t = dram("self_t", (NP, D))
    y_t = dram("y_t", (2 * NP, D))
    pa_t = dram("pa_t", (NP + P, D))
    pb_t = dram("pb_t", (NP + P, H))
    node_t = dram("node_t", (NP, 2))

    def rows_of(t, b):
        return t[at(b, BLK), :].rearrange("(p u) d -> p (u d)", u=U)

    def at(b, size=1):
        return bass.ds(b * size, size)

    def lagged(eng, *stages):
        deepest = max(lag for lag, _ in stages)
        assert deepest <= R

        def body(i):
            for s in range(R):
                if isinstance(i, int) and R * i + s >= NB:
                    break
                for lag, stage in stages:
                    b = R * i + s - lag
                    if not (isinstance(b, int) and b < 0):
                        q = (s - lag) % R
                        stage(b, q, i - (q - s + lag) // R)

        peeled_loop(eng, NI, body)
        for t in range(NB, NB + deepest):
            for lag, stage in stages:
                if t - lag < NB:
                    stage(t - lag, (t - lag) % R, (t - lag) // R)

    def in_pass(s):
        return len(range(s, NB, R))

    def uses(s, i):
        return 2 * i + s // 2

    def load_x(sp, tile, b, s, done):
        if isinstance(b, int) and b == FULL:
            sp.dma_start(tile[0:TAIL, s, 0:U * D], x[b * BLK:N, :].rearrange("(p u) d -> p (u d)", u=U))\
                .then_inc(done, 16)
        else:
            sp.dma_start(tile[:, s, 0:U * D], rows_of(x, b)).then_inc(done, 16)

    def accumulate(pe, o, products):
        for n, (lhsT, rhs) in enumerate(products):
            mm = pe.matmul(o, lhsT, rhs, start=(n == 0), stop=(n == len(products) - 1))
        return mm

    with ExitStack() as ctx:
        def sb(name, shape, dt=F32):
            return ctx.enter_context(nc.sbuf_tensor(name, shape, dt))

        phase = []

        def sem(name):
            return phase[0].enter_context(nc.semaphore(name))

        def run(make_phase, *args):
            with ExitStack() as semaphores:
                phase[:] = [semaphores]
                make_phase(*args)

        gathered = [ctx.enter_context(nc.semaphore(f"gathered{s}")) for s in range(R)]
        staged = ctx.enter_context(nc.semaphore("staged"))
        lasts_in, firsts_in, carried, carry_added, firsts_stored = (
            ctx.enter_context(nc.semaphore(name))
            for name in ("lasts_in", "firsts_in", "carried", "carry_added", "firsts_stored"))

        def gathers(nth, s, i):
            return 16 * U * (in_pass(s) * nth + i)

        bank = [ctx.enter_context(nc.psum_tensor(f"bank{i}", [P, 512], F32)) for i in range(8)]

        ident = sb("ident", [P, P])
        ones = sb("ones", [P, P])
        iota_f = sb("iota_f", [P, P])
        slot_T = sb("slot_T", [P, NB, U])
        src_T = sb("src_T", [P, NB, U], I32)
        srcy_T = sb("srcy_T", [P, NB, U], I32)
        M = sb("M", [NB, U, U, NB])
        tlast_i = sb("tlast_i", [NB, U], I32)
        node_row = sb("node_row", [P, NB, U], I32)
        node_inv = sb("node_inv", [P, NB, U])
        W0h = sb("W0h", [P, 2, H], F32R)
        W0l = sb("W0l", [P, 2, H], F32R)
        W1h = sb("W1h", [P, 2, K, H], F32R)
        W1l = sb("W1l", [P, 2, K, H], F32R)
        Wl2_r = sb("Wl2_r", [P, K, 2 * D], F32R)
        Wr2_r = sb("Wr2_r", [P, K, 2 * D], F32R)
        W3h = sb("W3h", [P, 3 * D], F32R)
        W3l = sb("W3l", [P, 3 * D], F32R)
        BIASES = 2 * H + 3 * D
        bias = sb("bias", [2, BIASES], F32R)
        bias0, bias1 = bias[:, 0:H], bias[:, H:2 * H]
        bias3 = bias[:, 2 * H:BIASES]
        b2_bc = sb("b2_bc", [P, U, D])
        ones_r = sb("ones_r", [2, P], F32R)
        sidx_T = sb("sidx_T", [P, NB, U], I32)
        payload_T = sb("payload_T", [P, NB, U, 2])
        signal = sb("signal", [P, 1])
        eps_c = sb("eps_c", [P, 1])

        def prepare(scratch):
            def sb(name, shape, dt=F32):
                return scratch.enter_context(nc.sbuf_tensor(name, shape, dt))

            dst_i = sb("dst_i", [NB, BLK], I32)
            next_i = sb("next_i", [NB, BLK], I32)
            src_i = sb("src_i", [NB, BLK], I32)
            typ_i = sb("typ_i", [NB, BLK], I32)
            dst_f = sb("dst_f", [NB, U, P])
            next_f = sb("next_f", [NB, U, P])
            src_f = sb("src_f", [NB, U, P])
            typ_f = sb("typ_f", [NB, U, P])
            pos = sb("pos", [NB, U, P])
            rbase = sb("rbase", [NB, U, P])
            e_idx = sb("e_idx", [NB, U, NB])
            k_idx = sb("k_idx", [NB, U])
            same = sb("same", [NB, U, P])
            starts = sb("starts", [NB, U, P])
            slot = sb("slot", [NB, U, P])
            row = sb("row", [NB, U, P])
            count = sb("count", [NB, U, P])
            first_run = sb("first_run", [NB, U, P])
            sidx = sb("sidx", [NB, U, P])
            srcy = sb("srcy", [NB, U, P])
            last_count = sb("last_count", [NB, U])
            diag = sb("diag", [NB, U, NB])
            hit = sb("hit", [NB, U, NB])
            zeros = sb("zeros", [P, H])
            fill = sb("fill", [P, NP // P, 2])
            w0 = sb("w0", [P, 2, H])
            w1 = sb("w1", [P, 2, K, H])
            w2 = sb("w2", [P, K, 2 * D])
            w3 = sb("w3", [P, 3 * D])
            bias_f = sb("bias_f", [2, BIASES])
            bias_h = sb("bias_h", [2, BIASES], F32R)
            bias_l = sb("bias_l", [2, BIASES])

            consts = sem("pr_consts")
            pads = sem("pr_pads")
            rows_in = sem("pr_rows_in")
            w_in = sem("pr_w_in")
            filled = sem("pr_filled")
            eye = sem("pr_eye")
            step = sem("pr_step")
            diag_ready = sem("pr_diag_ready")
            bc_ready = sem("pr_bc_ready")
            m_ready = sem("pr_m_ready")
            carry_ready = sem("pr_carry_ready")
            arrays_ready = sem("pr_arrays_ready")
            turned = sem("pr_turned")
            w3_turned = sem("pr_w3_turned")
            w_hi = sem("pr_w_hi")

            row_loads = [(dst_i, dst, 0), (next_i, dst, 1), (src_i, src, 0), (typ_i, etype, 0)]
            whole = E_FULL * BLK
            with nc.Block() as block:

                @block.gpsimd
                def _(pool):
                    pool.memset(dst_i[:, :], PAD_DST).then_inc(pads, 1)
                    pool.memset(next_i[:, :], PAD_DST).then_inc(pads, 1)
                    pool.memset(src_i[:, :], 0).then_inc(pads, 1)
                    pool.memset(typ_i[:, :], 0).then_inc(pads, 1)
                    pool.memset(zeros[:, :], 0.0).then_inc(consts, 1)
                    pool.memset(fill[:, :, 0], float(ZROW)).then_inc(consts, 1)
                    pool.memset(fill[:, :, 1], 1.0).then_inc(consts, 1)
                    pool.memset(ident[:, :], 0.0).then_inc(eye, 1)
                    pool.memset(ones[:, :], 1.0).then_inc(consts, 1)
                    pool.memset(eps_c[:, :], EPS).then_inc(consts, 1)
                    pool.wait_ge(eye, 1)
                    pool.affine_select(out=ident[:, :], in_=ident[:, :], compare_op=ALU.not_equal, fill=1.0,
                                       base=0, pattern=[[-1, P]], channel_multiplier=1).then_inc(consts, 1)
                    ok = dict(allow_small_or_imprecise_dtypes=True)
                    pool.iota(iota_f[:, :], [[1, P]], base=0, channel_multiplier=0, **ok).then_inc(consts, 1)
                    pool.iota(pos[:, :, :], [[0, U], [1, P]], base=0, channel_multiplier=0, **ok).then_inc(consts, 1)
                    pool.iota(rbase[:, :, :], [[1, U], [0, P]], base=0, channel_multiplier=BLK, **ok)\
                        .then_inc(consts, 1)
                    pool.iota(e_idx[:, :, :], [[1, U], [U, NB]], base=0, channel_multiplier=0, **ok)\
                        .then_inc(consts, 1)
                    pool.iota(k_idx[:, :], [[1, U]], base=0, channel_multiplier=U, **ok).then_inc(consts, 1)

                ALL_CONSTS = 11

                @block.sync
                def _(sp):
                    sp.wait_ge(pads, 4)
                    for tile, array, off in row_loads:
                        left = E - whole - off
                        sp.dma_start(tile[0:E_FULL, :],
                                     array[off:off + whole].rearrange("(b i) -> b i", i=BLK)).then_inc(rows_in, 16)
                        sp.dma_start(tile[E_FULL:E_FULL + 1, 0:left],
                                     array[off + whole:off + whole + left].rearrange("(a i) -> a i", a=1))\
                            .then_inc(rows_in, 16)
                    sp.dma_start(w0[:, 0, :], Wl0).then_inc(w_in, 16)
                    sp.dma_start(w0[:, 1, :], Wr0).then_inc(w_in, 16)
                    sp.dma_start(w1[:, 0, :, :], Wl1.rearrange("(k p) n -> p k n", p=P)).then_inc(w_in, 16)
                    sp.dma_start(w1[:, 1, :, :], Wr1.rearrange("(k p) n -> p k n", p=P)).then_inc(w_in, 16)
                    sp.dma_start(w2[:, :, 0:D], Wl2.rearrange("(k p) n -> p k n", p=P)).then_inc(w_in, 16)
                    sp.dma_start(w2[:, :, D:2 * D], Wr2.rearrange("(k p) n -> p k n", p=P)).then_inc(w_in, 16)
                    for n, w in enumerate((Wd, Wc, Ws)):
                        sp.dma_start(w3[:, n * D:(n + 1) * D], w).then_inc(w_in, 16)
                    place = 0
                    for b in (b0, b1, bd, bc, bs):
                        n = b.shape[0]
                        sp.dma_start(bias_f[:, place:place + n], b.rearrange("(a n) -> a n", a=1).to_broadcast([2, n]))\
                            .then_inc(w_in, 16)
                        place += n
                    for u in range(U):
                        sp.dma_start(b2_bc[:, u, :], b2.rearrange("(a n) -> a n", a=1).to_broadcast([P, D]))\
                            .then_inc(w_in, 16)
                    sp.wait_ge(consts, ALL_CONSTS)
                    sp.dma_start(pa_t[NP:NP + P, :], zeros[:, 0:D]).then_inc(filled, 16)
                    sp.dma_start(pb_t[NP:NP + P, :], zeros[:, :]).then_inc(filled, 16)
                    sp.dma_start(node_t.rearrange("(p k) v -> p (k v)", p=P),
                                 fill[:, :, :].rearrange("p k v -> p (k v)")).then_inc(filled, 16)
                    sp.wait_ge(filled, 48)

                N_W = 16 * (9 + 5 + U)

                @block.scalar
                def _(act):
                    act.wait_ge(w_in, N_W)
                    act.activation(W0h[:, :, :], w0[:, :, :], ACT.Copy).then_inc(w_hi, 1)
                    act.activation(W1h[:, :, :, :].rearrange("p a b c -> p (a b c)"),
                                   w1[:, :, :, :].rearrange("p a b c -> p (a b c)"), ACT.Copy).then_inc(w_hi, 1)
                    act.activation(Wl2_r[:, :, 0:D], w2[:, :, 0:D], ACT.Copy).then_inc(w_hi, 1)
                    act.activation(Wr2_r[:, :, 0:D], w2[:, :, D:2 * D], ACT.Copy).then_inc(w_hi, 1)
                    act.wait_ge(w3_turned, 1)
                    act.activation(W3h[:, :], bank[6][:, 0:3 * D], ACT.Copy).then_inc(w_hi, 1)

                arrays = [(slot, slot_T[:, :, :]), (src_f, src_T[:, :, :]), (srcy, srcy_T[:, :, :]),
                          (sidx, sidx_T[:, :, :]), (row, payload_T[:, :, :, 0]), (count, payload_T[:, :, :, 1])]

                @block.vector
                def _(dve):
                    done = [0]

                    def chain(ins):
                        done[0] += 1
                        ins.then_inc(step, 1)

                    def settle():
                        dve.wait_ge(step, done[0])

                    flat = "b u i -> b (u i)"
                    dve.wait_ge(rows_in, 16 * 8)
                    dve.wait_ge(consts, ALL_CONSTS)
                    for f, i in ((dst_f, dst_i), (next_f, next_i), (src_f, src_i), (typ_f, typ_i)):
                        chain(dve.tensor_copy(f[:, :, :].rearrange(flat), i[:, :]))
                    chain(dve.memset(same[:, :, :], 0.0))
                    settle()
                    chain(dve.tensor_tensor(same[:, :, 1:P], dst_f[:, :, 1:P], dst_f[:, :, 0:P - 1], ALU.is_equal))
                    for u in range(U):
                        chain(dve.tensor_scalar(diag[:, u, :], ident[0:NB, 0:NB], dst_f[:, u, 0:1], None, ALU.mult))
                    settle()
                    dve.tensor_copy(signal[:, :], ident[:, 0:1]).then_inc(diag_ready, 1)
                    chain(dve.tensor_scalar(starts[:, :, :], same[:, :, :], -1.0, 1.0, ALU.mult, ALU.add))
                    settle()
                    chain(dve.tensor_tensor(starts[:, :, :], starts[:, :, :], pos[:, :, :], ALU.mult))
                    settle()
                    chain(dve.tensor_tensor_scan(slot[:, :, :].rearrange(flat), same[:, :, :].rearrange(flat),
                                                 starts[:, :, :].rearrange(flat), 0.0, ALU.mult, ALU.add))
                    settle()
                    chain(dve.scalar_tensor_tensor(row[:, :, :], slot[:, :, :], float(U), rbase[:, :, :],
                                                   ALU.mult, ALU.add))
                    chain(dve.scalar_tensor_tensor(count[:, :, :], pos[:, :, :], 1.0, slot[:, :, :],
                                                   ALU.add, ALU.subtract))
                    chain(dve.tensor_scalar(first_run[:, :, :], slot[:, :, :], 0.0, None, ALU.is_equal))
                    chain(dve.tensor_scalar(last_count[:, :], slot[:, :, P - 1], -1.0, float(P), ALU.mult, ALU.add))
                    chain(dve.tensor_tensor(sidx[:, :, :], dst_f[:, :, :], next_f[:, :, :], ALU.is_equal))
                    chain(dve.tensor_scalar(typ_f[:, :, :], typ_f[:, :, :], 0.0, None, ALU.is_equal))
                    settle()
                    chain(dve.tensor_copy(tlast_i[:, :], row[:, :, P - 1]))
                    chain(dve.tensor_scalar(sidx[:, :, :], sidx[:, :, :], -1.0, 1.0, ALU.mult, ALU.add))
                    chain(dve.scalar_tensor_tensor(srcy[:, :, :], typ_f[:, :, :], -float(NP), src_f[:, :, :],
                                                   ALU.mult, ALU.add))
                    settle()
                    chain(dve.tensor_scalar(srcy[:, :, :], srcy[:, :, :], float(NP), None, ALU.add))
                    chain(dve.scalar_tensor_tensor(sidx[:, :, :], dst_f[:, :, :], -float(PAD_DST), sidx[:, :, :],
                                                   ALU.add, ALU.mult))
                    settle()
                    chain(dve.tensor_scalar(sidx[:, :, :], sidx[:, :, :], float(PAD_DST), None, ALU.add))
                    dve.wait_ge(bc_ready, 1)
                    bcast = bank[6][0:NB, 0:U * NB].rearrange("k (u b) -> k u b", u=U)
                    for u in range(U):
                        chain(dve.tensor_scalar(hit[:, :, :], bcast, dst_f[:, u, P - 1:P], None, ALU.is_equal))
                        settle()
                        chain(dve.scalar_tensor_tensor(M[:, u, :, :], e_idx[:, :, :], k_idx[:, u:u + 1],
                                                       hit[:, :, :], ALU.is_gt, ALU.mult))
                        settle()
                    dve.tensor_copy(signal[:, :], ident[:, 0:1]).then_inc(m_ready, 1)
                    dve.wait_ge(carry_ready, 1)
                    for u in range(U):
                        chain(dve.scalar_tensor_tensor(count[:, u, :], first_run[:, u, :], bank[7][0:NB, u:u + 1],
                                                       count[:, u, :], ALU.mult, ALU.add))
                    settle()
                    dve.tensor_copy(signal[:, :], ident[:, 0:1]).then_inc(arrays_ready, 1)
                    for n, (_, table) in enumerate(arrays):
                        dve.wait_ge(turned, n + 1)
                        chain(dve.tensor_copy(table.rearrange("p b u -> p u b"),
                                              bank[n][:, 0:U * NB].rearrange("p (u b) -> p u b", u=U)))
                    dve.wait_ge(w_hi, 5)
                    dve.tensor_tensor(W0l[:, :, :], w0[:, :, :], W0h[:, :, :].bitcast(F32), ALU.subtract)
                    dve.tensor_tensor(W1l[:, :, :, :].rearrange("p a b c -> p (a b c)"),
                                      w1[:, :, :, :].rearrange("p a b c -> p (a b c)"),
                                      W1h[:, :, :, :].rearrange("p a b c -> p (a b c)").bitcast(F32), ALU.subtract)
                    dve.tensor_tensor(Wl2_r[:, :, D:2 * D], w2[:, :, 0:D], Wl2_r[:, :, 0:D].bitcast(F32), ALU.subtract)
                    dve.tensor_tensor(Wr2_r[:, :, D:2 * D], w2[:, :, D:2 * D], Wr2_r[:, :, 0:D].bitcast(F32),
                                      ALU.subtract)
                    chain(dve.tensor_copy(ones_r[:, :], ones[0:2, :]))
                    chain(dve.tensor_copy(bias_h[:, :], bias_f[:, :]))
                    settle()
                    chain(dve.tensor_tensor(bias_l[:, :], bias_f[:, :], bias_h[:, :].bitcast(F32), ALU.subtract))
                    settle()
                    chain(dve.tensor_scalar(bias_l[:, :], bias_l[:, :], ident[0:2, 1:2], None, ALU.mult))
                    settle()
                    dve.scalar_tensor_tensor(bias[:, :], bias_h[:, :].bitcast(F32), ident[0:2, 0:1], bias_l[:, :],
                                             ALU.mult, ALU.add)
                    dve.tensor_tensor(W3l[:, :], bank[6][:, 0:3 * D], W3h[:, :].bitcast(F32), ALU.subtract)

                @block.tensor
                def _(pe):
                    pe.wait_ge(consts, ALL_CONSTS)
                    pe.wait_ge(diag_ready, 1)
                    for u in range(U):
                        mm = pe.matmul(bank[6][0:NB, u * NB:(u + 1) * NB], ones[0:NB, 0:NB], diag[:, u, :],
                                       start=True, stop=True)
                    mm.then_inc(bc_ready, 1)
                    pe.wait_ge(m_ready, 1)
                    for e in range(U):
                        for k in range(U):
                            mm = pe.matmul(bank[7][0:NB, e:e + 1], M[:, k, e, :], last_count[:, k:k + 1],
                                           start=(k == 0), stop=(k == U - 1))
                    mm.then_inc(carry_ready, 1)
                    pe.wait_ge(w_in, N_W)
                    for n in range(3):
                        mm = pe.transpose(bank[6][:, n * D:(n + 1) * D], w3[:, n * D:(n + 1) * D], ident[:, :])
                    mm.then_inc(w3_turned, 1)
                    pe.wait_ge(arrays_ready, 1)
                    for n, (array, _) in enumerate(arrays):
                        for u in range(U):
                            mm = pe.transpose(bank[n][:, u * NB:(u + 1) * NB], array[:, u, :], ident[0:NB, 0:NB])
                        mm.then_inc(turned, 1)

        def ln_stats(dve, rows, s, step, done):
            for u in range(U):
                dve.bn_stats(stats[:, s, u, :], rows[:, u, :]).then_inc(step, 1)
            dve.wait_ge(step, done + U)
            dve.nop(nofuse=True)
            for u in range(U):
                last = dve.bn_aggr(mv[:, s, u, :], stats[:, s, u, :])
            return last

        def ln_scalars(dve, s, b, std_ready, rstd_ready):
            dve.wait_ge(std_ready, b + 1)
            dve.reciprocal(rstd[:, s, :], std[:, s, :]).then_inc(rstd_ready, 1)
            dve.wait_ge(rstd_ready, 2 * b + 1)
            dve.scalar_tensor_tensor(nbias[:, s, :], mv[:, s, :, 0], -1.0, rstd[:, s, :],
                                     ALU.mult, ALU.mult).then_inc(rstd_ready, 1)

        def layer_norm_x():
            x_in = [sem(f"ln_x_in{s}") for s in range(R)]
            stored = [sem(f"ln_stored{s}") for s in range(2)]
            xb_ready = sem("ln_xb")
            xb_stored = [sem(f"ln_xb_stored{s}") for s in range(R)]
            step = sem("ln_step")
            mean_var = sem("ln_mean_var")
            std_ready = sem("ln_std")
            rstd_ready = sem("ln_rstd")
            h_ready = sem("ln_h")
            staged = sem("ln_staged")
            scattered = [sem(f"ln_scattered{s}") for s in range(R)]
            with nc.Block() as block:

                @block.sync
                def _(sp):
                    def load(b, s, i):
                        wait(sp, h_ready, b - R + 1)
                        wait(sp, xb_ready, b - R + 1)
                        load_x(sp, own, b, s, x_in[s])

                    def store_xb(b, s, i):
                        sp.wait_ge(xb_ready, b + 1)
                        sp.dma_start(rows_of(xb_t, b), own[:, s, U * D:2 * U * D]).then_inc(xb_stored[s], 16)

                    lagged(sp, (3, store_xb), (0, load))
                    for s in range(R):
                        sp.wait_ge(xb_stored[s], 16 * in_pass(s))

                @block.vector
                def _(dve):
                    def statistics(b, s, i):
                        dve.wait_ge(x_in[s], 16 * (i + 1))
                        wait(dve, h_ready, b - R + 1)
                        rows = own[:, s, 0:U * D].rearrange("p (u d) -> p u d", u=U)
                        ln_stats(dve, rows, s, step, U * b).then_inc(mean_var, 1)

                    def scalars(b, s, i):
                        ln_scalars(dve, s, b, std_ready, rstd_ready)

                    def add_b2(b, s, i):
                        wait(dve, xb_stored[s], 16 * i)
                        dve.tensor_tensor(own[:, s, U * D:2 * U * D], own[:, s, 0:U * D],
                                          b2_bc[:, :, :].rearrange("p u d -> p (u d)"), ALU.add).then_inc(xb_ready, 1)

                    lagged(dve, (0, statistics), (0, add_b2), (1, scalars))

                @block.scalar
                def _(act):
                    def deviation(b, s, i):
                        act.wait_ge(mean_var, b + 1)
                        act.activation(std[:, s, :], mv[:, s, :, 1], ACT.Sqrt, bias=eps_c[:, 0:1])\
                            .then_inc(std_ready, 1)

                    def apply(b, s, i):
                        act.wait_ge(rstd_ready, 2 * b + 2)
                        wait(act, stored[s % 2], 16 * uses(s, i))
                        for u in range(U):
                            last = act.activation(res[:, s % 2, u * D:(u + 1) * D], own[:, s, u * D:(u + 1) * D],
                                                  ACT.Relu, bias=nbias[:, s, u:u + 1], scale=rstd[:, s, u:u + 1])
                        last.then_inc(h_ready, 1)

                    def store(b, s, i):
                        act.wait_ge(h_ready, b + 1)
                        act.dma_start(rows_of(h0_t, b), res[:, s % 2, 0:U * D]).then_inc(stored[s % 2], 16)

                    lagged(act, (0, deviation), (1, apply), (2, store))
                    for s in range(2):
                        act.wait_ge(stored[s], 16 * (NB // 2))

                @block.gpsimd
                def _(pool):
                    def scatter(b, s, i):
                        wait(pool, scattered[s], 16 * U * i)
                        pool.tensor_copy(stage[:, s, :], sidx_T[:, at(b), :].rearrange("p a u -> p (a u)"))\
                            .then_inc(staged, 1)
                        pool.tensor_copy(pay_stage[:, s, :], payload_T[:, at(b), :, :].rearrange(
                            "p a u v -> p (a u v)")).then_inc(staged, 1)
                        pool.wait_ge(staged, 2 * b + 2)
                        pool.nop(nofuse=True)
                        for u in range(U):
                            pool.indirect_dma_start(
                                node_t, bass.IndirectOffsetOnAxis(stage[:, s, u:u + 1], 0),
                                pay_stage[:, s, 2 * u:2 * u + 2], None,
                                bounds_check=NP - 1, oob_is_err=False).then_inc(scattered[s], 16)

                    lagged(pool, (0, scatter))
                    for s in range(R):
                        pool.wait_ge(scattered[s], 16 * U * in_pass(s))

        def load_node_entries():
            entries = sb("entries", [P, NB, U, 2])
            loaded = sem("ne_loaded")
            split = sem("ne_split")
            with nc.Block() as block:

                @block.sync
                def _(sp):
                    sp.dma_start(entries[:, :, :, :].rearrange("p b u v -> p b (u v)"),
                                 node_t.rearrange("(b p u) v -> p b (u v)", p=P, u=U)).then_inc(loaded, 16)

                @block.vector
                def _(dve):
                    dve.wait_ge(loaded, 16)
                    dve.tensor_copy(node_row[:, :, :], entries[:, :, :, 0]).then_inc(split, 1)
                    dve.reciprocal(node_inv[:, :, :], entries[:, :, :, 1]).then_inc(split, 1)

        def gather_blocks(pool, table, index, width, nth, freed):
            def gather(b, s, i):
                if s % 2 == 0:
                    wait(pool, gathered[s], gathers(nth, s, i))
                    wait(pool, gathered[s + 1], gathers(nth, s + 1, i))
                    pool.tensor_copy(stage[:, s:s + 2, :], index[:, bass.ds(b, 2), :]).then_inc(staged, 1)
                wait(pool, freed, b - R + 1)
                pool.wait_ge(staged, NB // 2 * nth + 2 * i + s // 2 + 1)
                pool.nop(nofuse=True)
                for u in range(U):
                    pool.indirect_dma_start(raw[:, s, u * width:(u + 1) * width], None, table,
                                            bass.IndirectOffsetOnAxis(stage[:, s, u:u + 1], 0))\
                        .then_inc(gathered[s], 16)

            lagged(pool, (0, gather))

        def run_sums(tag, nth, width, table, index, p_t):
            n_banks = width * U // 512
            hi = sem(tag + "_hi")
            lo = sem(tag + "_lo")
            onehot = sem(tag + "_onehot")
            summed = sem(tag + "_summed")
            out_a = sem(tag + "_out_a")
            out_v = sem(tag + "_out_v")
            stored = [sem(f"{tag}_stored{s}") for s in range(2)]
            size = U * width
            with nc.Block() as block:

                @block.gpsimd
                def _(pool):
                    gather_blocks(pool, table, index, width, nth, lo)

                @block.scalar
                def _(act):
                    def upper(b, s, i):
                        act.wait_ge(gathered[s], gathers(nth, s, i + 1))
                        wait(act, summed, b - 1)
                        act.activation(big_h[:, s % 2, 0:size], raw[:, s, 0:size], ACT.Copy).then_inc(hi, 1)

                    def evacuate(b, s, i):
                        act.wait_ge(summed, b + 1)
                        wait(act, stored[s % 2], 16 * uses(s, i))
                        act.activation(res[:, s % 2, 0:512], bank[s * n_banks][:, :], ACT.Copy).then_inc(out_a, 1)

                    lagged(act, (0, upper), (1, evacuate))

                @block.vector
                def _(dve):
                    def split(b, s, i):
                        wait(dve, summed, b - 1)
                        for u in range(U):
                            last = dve.tensor_scalar(S[:, s % 2, u, :], iota_f[:, :],
                                                     slot_T[:, at(b), u:u + 1].rearrange("p a u -> p (a u)"),
                                                     None, ALU.is_equal)
                        last.then_inc(onehot, 1)
                        dve.wait_ge(gathered[s], gathers(nth, s, i + 1))
                        dve.wait_ge(hi, b + 1)
                        dve.tensor_tensor(big_l[:, s % 2, 0:size], raw[:, s, 0:size],
                                          big_h[:, s % 2, 0:size].bitcast(F32), ALU.subtract).then_inc(lo, 1)

                    def evacuate(b, s, i):
                        dve.wait_ge(summed, b + 1)
                        wait(dve, stored[s % 2], 16 * uses(s, i))
                        dve.tensor_copy(res[:, s % 2, 512:1024], bank[2 * s + 1][:, :]).then_inc(out_v, 1)

                    lagged(dve, (0, split), *([(1, evacuate)] if n_banks == 2 else []))

                @block.tensor
                def _(pe):
                    def add_up(b, s, i):
                        pe.wait_ge(onehot, b + 1)
                        pe.wait_ge(lo, b + 1)
                        wait(pe, out_a, b - R + 1)
                        if n_banks == 2:
                            wait(pe, out_v, b - R + 1)
                        for u in range(U):
                            c = u * width
                            o = bank[s * n_banks + c // 512][:, c % 512:c % 512 + width]
                            mm = accumulate(pe, o, [(S[:, s % 2, u, :], big_h[:, s % 2, c:c + width]),
                                                    (S[:, s % 2, u, :], big_l[:, s % 2, c:c + width])])
                        mm.then_inc(summed, 1)

                    lagged(pe, (0, add_up))

                @block.sync
                def _(sp):
                    def store(b, s, i):
                        sp.wait_ge(out_a, b + 1)
                        if n_banks == 2:
                            sp.wait_ge(out_v, b + 1)
                        sp.dma_start(rows_of(p_t, b), res[:, s % 2, 0:size]).then_inc(stored[s % 2], 16)

                    lagged(sp, (0, store))
                    for s in range(2):
                        sp.wait_ge(stored[s], 16 * (NB // 2))

        def transformed_sums(tag, nth, table, index, Wh, Wl, p_t, relu):
            width = H if Wl is not None else D
            halves = Wl is None
            n_banks = H * U // 512
            hi = sem(tag + "_hi")
            lo = sem(tag + "_lo")
            onehot = sem(tag + "_onehot")
            summed = sem(tag + "_summed")
            agg_hi = sem(tag + "_agg_hi")
            agg_lo = sem(tag + "_agg_lo")
            dense = sem(tag + "_dense")
            copied = sem(tag + "_copied")
            out = sem(tag + "_out") if halves else copied
            stored = [sem(f"{tag}_stored{s}") for s in range(2)]
            size = U * width
            with nc.Block() as block:

                @block.gpsimd
                def _(pool):
                    gather_blocks(pool, table, index, H, nth, lo)

                @block.scalar
                def _(act):
                    def upper(b, s, i):
                        act.wait_ge(gathered[s], gathers(nth, s, i + 1))
                        wait(act, summed, b - 1)
                        act.activation(big_h[:, s % 2, :], raw[:, s, :], ACT.Relu if relu else ACT.Copy)\
                            .then_inc(hi, 1)

                    def upper_sums(b, s, i):
                        act.wait_ge(summed, b + 1)
                        wait(act, dense, b - 1)
                        for k in range(K):
                            act.activation(own_h[:, s % 2, k * 512:(k + 1) * 512], bank[2 * (s % 2) + k][:, :],
                                           ACT.Copy).then_inc(agg_hi, 1)

                    def evacuate(b, s, i):
                        q = s % 2
                        act.wait_ge(dense, b + 1)
                        if not halves:
                            wait(act, stored[q], 16 * uses(s, i))
                        else:
                            wait(act, out, b - 1)
                        for n in range(n_banks):
                            if halves:
                                last = act.activation(half[:, q, n * 2:n * 2 + 2, :],
                                                      bank[4 + 2 * q + n][:, :].rearrange(
                                                          "p (u g d) -> p u g d", u=2, g=2)[:, :, 1, :], ACT.Copy)
                            else:
                                last = act.activation(res[:, q, n * 512:(n + 1) * 512],
                                                      bank[4 + 2 * q + n][:, :], ACT.Copy)
                        last.then_inc(copied, 1)

                    lagged(act, (0, upper), (1, upper_sums), (2, evacuate))

                @block.vector
                def _(dve):
                    def split(b, s, i):
                        wait(dve, summed, b - 1)
                        for u in range(U):
                            last = dve.tensor_scalar(S[:, s % 2, u, :], iota_f[:, :],
                                                     slot_T[:, at(b), u:u + 1].rearrange("p a u -> p (a u)"),
                                                     None, ALU.is_equal)
                        last.then_inc(onehot, 1)
                        dve.wait_ge(gathered[s], gathers(nth, s, i + 1))
                        dve.wait_ge(hi, b + 1)
                        upper = big_h[:, s % 2, :].bitcast(F32)
                        if relu:
                            dve.scalar_tensor_tensor(big_l[:, s % 2, :], raw[:, s, :], 0.0, upper,
                                                     ALU.max, ALU.subtract).then_inc(lo, 1)
                        else:
                            dve.tensor_tensor(big_l[:, s % 2, :], raw[:, s, :], upper, ALU.subtract).then_inc(lo, 1)

                    def lower_sums(b, s, i):
                        wait(dve, dense, b - 1)
                        for k in range(K):
                            dve.wait_ge(agg_hi, K * b + k + 1)
                            c = slice(k * 512, (k + 1) * 512)
                            dve.tensor_tensor(own_l[:, s % 2, c], bank[2 * (s % 2) + k][:, :],
                                              own_h[:, s % 2, c].bitcast(F32), ALU.subtract).then_inc(agg_lo, 1)

                    def add_halves(b, s, i):
                        q = s % 2
                        dve.wait_ge(copied, b + 1)
                        wait(dve, stored[q], 16 * uses(s, i))
                        for n in range(n_banks):
                            last = dve.tensor_tensor(
                                res[:, q, n * 2 * D:(n + 1) * 2 * D].rearrange("p (u d) -> p u d", u=2),
                                bank[4 + 2 * q + n][:, :].rearrange("p (u g d) -> p u g d", u=2, g=2)[:, :, 0, :],
                                half[:, q, n * 2:n * 2 + 2, :], ALU.add)
                        last.then_inc(out, 1)

                    lagged(dve, *([(3, add_halves)] if halves else []), (0, split), (1, lower_sums))

                @block.tensor
                def _(pe):
                    def add_up(b, s, i):
                        pe.wait_ge(onehot, b + 1)
                        pe.wait_ge(lo, b + 1)
                        wait(pe, agg_lo, K * (b - 1))
                        for k in range(K):
                            for u in range(U):
                                c = slice(u * H + k * P, u * H + (k + 1) * P)
                                mm = accumulate(pe, bank[2 * (s % 2) + k][:, u * P:(u + 1) * P],
                                                [(big_h[:, s % 2, c], S[:, s % 2, u, :]),
                                                 (big_l[:, s % 2, c], S[:, s % 2, u, :])])
                        mm.then_inc(summed, 1)

                    def product(b, s, i):
                        q = s % 2
                        pe.wait_ge(agg_lo, K * (b + 1))
                        wait(pe, out, b - 1)
                        for u in range(U):
                            products = []
                            for k in range(K):
                                c = slice(k * 512 + u * P, k * 512 + (u + 1) * P)
                                products += [(own_h[:, q, c], Wh[:, k, :]), (own_l[:, q, c], Wh[:, k, :])]
                                if not halves:
                                    products.append((own_h[:, q, c], Wl[:, k, :]))
                            mm = accumulate(pe, bank[4 + 2 * q + u // 2][:, (u % 2) * H:(u % 2 + 1) * H], products)
                        mm.then_inc(dense, 1)

                    lagged(pe, (0, add_up), (1, product))

                @block.sync
                def _(sp):
                    def store(b, s, i):
                        sp.wait_ge(out, b + 1)
                        sp.dma_start(rows_of(p_t, b), res[:, s % 2, 0:size]).then_inc(stored[s % 2], 16)

                    lagged(sp, (0, store))
                    for s in range(2):
                        sp.wait_ge(stored[s], 16 * (NB // 2))

        def carry_runs(nth, width, p_t):
            firsts = p_t[0:NP, :].rearrange("(b q) d -> b (q d)", q=BLK)[:, 0:U * width]
            n_banks = width * U // 512
            with nc.Block() as block:

                @block.gpsimd
                def _(pool):
                    for u in range(U):
                        pool.indirect_dma_start(raw[0:NB, 0, u * width:(u + 1) * width], None, p_t,
                                                bass.IndirectOffsetOnAxis(tlast_i[:, u:u + 1], 0))\
                            .then_inc(lasts_in, 16)

                @block.sync
                def _(sp):
                    sp.dma_start(own[0:NB, 0, 0:U * width], firsts).then_inc(firsts_in, 16)
                    sp.wait_ge(carry_added, nth + 1)
                    sp.dma_start(firsts, res[0:NB, 0, 0:U * width]).then_inc(firsts_stored, 16)
                    sp.wait_ge(firsts_stored, 16 * (nth + 1))

                @block.tensor
                def _(pe):
                    pe.wait_ge(lasts_in, 16 * U * (nth + 1))
                    for e in range(U):
                        c = e * width
                        for k in range(U):
                            mm = pe.matmul(bank[c // 512][0:NB, c % 512:c % 512 + width], M[:, k, e, :],
                                           raw[0:NB, 0, k * width:(k + 1) * width],
                                           start=(k == 0), stop=(k == U - 1))
                    mm.then_inc(carried, 1)

                @block.vector
                def _(dve):
                    dve.wait_ge(firsts_in, 16 * (nth + 1))
                    dve.wait_ge(carried, nth + 1)
                    for n in range(n_banks):
                        last = dve.tensor_tensor(res[0:NB, 0, n * 512:(n + 1) * 512],
                                                 own[0:NB, 0, n * 512:(n + 1) * 512], bank[n][0:NB, :], ALU.add)
                    last.then_inc(carry_added, 1)

        def mean_rows(dve, b, s, width, nth, i, scaled):
            dve.wait_ge(gathered[s], gathers(nth, s, i + 1))
            for u in range(U):
                c = slice(u * width, (u + 1) * width)
                last = dve.tensor_scalar(raw[:, s, c], raw[:, s, c],
                                         node_inv[:, at(b), u:u + 1].rearrange("p a u -> p (a u)"), None, ALU.mult)
            last.then_inc(scaled, 1)

        def sage_0(nth):
            own_in = [sem(f"b0_own_in{s}") for s in range(R)]
            stored = [sem(f"b0_stored{s}") for s in range(2)]
            scaled = sem("b0_scaled")
            turned = sem("b0_turned")
            hi = sem("b0_hi")
            lo = sem("b0_lo")
            dense = sem("b0_dense")
            h_ready = sem("b0_h")
            with nc.Block() as block:

                @block.gpsimd
                def _(pool):
                    gather_blocks(pool, pa_t, node_row, D, nth, turned)

                @block.sync
                def _(sp):
                    def load(b, s, i):
                        wait(sp, turned, b - R + 1)
                        sp.dma_start(own[:, s, 0:U * D], rows_of(h0_t, b)).then_inc(own_in[s], 16)

                    lagged(sp, (0, load))

                @block.vector
                def _(dve):
                    def scale(b, s, i):
                        mean_rows(dve, b, s, D, nth, i, scaled)

                    def lower(b, s, i):
                        dve.wait_ge(hi, b + 1)
                        wait(dve, dense, b - 1)
                        q = s % 2
                        dve.tensor_tensor(big_l[:, q, 0:512], bank[2 * q][:, :], big_h[:, q, 0:512].bitcast(F32),
                                          ALU.subtract)
                        dve.tensor_tensor(own_l[:, q, 0:512], bank[2 * q + 1][:, :],
                                          own_h[:, q, 0:512].bitcast(F32), ALU.subtract).then_inc(lo, 1)

                    lagged(dve, (0, scale), (1, lower))

                @block.scalar
                def _(act):
                    def upper(b, s, i):
                        act.wait_ge(turned, b + 1)
                        wait(act, dense, b - 1)
                        q = s % 2
                        act.activation(big_h[:, q, 0:512], bank[2 * q][:, :], ACT.Copy)
                        act.activation(own_h[:, q, 0:512], bank[2 * q + 1][:, :], ACT.Copy).then_inc(hi, 1)

                    def relu(b, s, i):
                        q = s % 2
                        act.wait_ge(dense, b + 1)
                        wait(act, stored[q], 16 * uses(s, i))
                        for n in range(2):
                            last = act.activation(res[:, q, n * 512:(n + 1) * 512], bank[4 + 2 * q + n][:, :],
                                                  ACT.Relu)
                        last.then_inc(h_ready, 1)

                    def store(b, s, i):
                        act.wait_ge(h_ready, b + 1)
                        act.dma_start(rows_of(h1_t, b), res[:, s % 2, :]).then_inc(stored[s % 2], 16)

                    lagged(act, (1, upper), (2, relu), (3, store))
                    for s in range(2):
                        act.wait_ge(stored[s], 16 * (NB // 2))

                @block.tensor
                def _(pe):
                    def turn(b, s, i):
                        pe.wait_ge(scaled, b + 1)
                        pe.wait_ge(own_in[s], 16 * (i + 1))
                        wait(pe, lo, b - 1)
                        for n, rows in enumerate((raw, own)):
                            for u in range(U):
                                mm = pe.transpose(bank[2 * (s % 2) + n][:, u * P:(u + 1) * P],
                                                  rows[:, s, u * D:(u + 1) * D], ident[:, :])
                        mm.then_inc(turned, 1)

                    def product(b, s, i):
                        pe.wait_ge(lo, b + 1)
                        wait(pe, h_ready, b - 1)
                        q = s % 2
                        for u in range(U):
                            c = slice(u * P, (u + 1) * P)
                            mm = accumulate(pe, bank[4 + 2 * q + u // 2][:, (u % 2) * H:(u % 2 + 1) * H], [
                                (ones_r[:, :], bias0),
                                (big_h[:, q, c], W0h[:, 0, :]), (big_h[:, q, c], W0l[:, 0, :]),
                                (big_l[:, q, c], W0h[:, 0, :]), (own_h[:, q, c], W0h[:, 1, :]),
                                (own_h[:, q, c], W0l[:, 1, :]), (own_l[:, q, c], W0h[:, 1, :])])
                        mm.then_inc(dense, 1)

                    lagged(pe, (1, turn), (2, product))

        def sage_1(nth):
            own_in = [sem(f"b1_own_in{s}") for s in range(R)]
            x_in = [sem(f"b1_x_in{s}") for s in range(R)]
            stored_r = [sem(f"b1_stored_r{s}") for s in range(2)]
            stored_s = [sem(f"b1_stored_s{s}") for s in range(2)]
            turned = sem("b1_turned")
            hi = sem("b1_hi")
            lo = sem("b1_lo")
            dense = sem("b1_dense")
            r_ready = sem("b1_r")
            r_turned = sem("b1_r_turned")
            h2_hi = sem("b1_h2_hi")
            h2_lo = sem("b1_h2_lo")
            dense2 = sem("b1_dense2")
            half_added = sem("b1_half_added")
            s_out = sem("b1_s_out")
            with nc.Block() as block:

                @block.gpsimd
                def _(pool):
                    gather_blocks(pool, pb_t, node_row, H, nth, r_ready)

                @block.sync
                def _(sp):
                    def load(b, s, i):
                        wait(sp, turned, b - R + 1)
                        sp.dma_start(own[:, s, :], rows_of(h1_t, b)).then_inc(own_in[s], 16)

                    def load_residual(b, s, i):
                        wait(sp, s_out, b - R + 1)
                        sp.dma_start(x1_b[:, s, :], rows_of(xb_t, b)).then_inc(x_in[s], 16)

                    lagged(sp, (0, load), (3, load_residual))

                @block.tensor
                def _(pe):
                    def product(b, s, i):
                        q = s % 2
                        pe.wait_ge(lo, K * (b + 1))
                        wait(pe, r_ready, b)
                        for u in range(U):
                            products = [(ones_r[:, :], bias1)]
                            for k in range(K):
                                c = slice(k * 512 + u * P, k * 512 + (u + 1) * P)
                                products += [(own_h[:, q, c], W1h[:, 1, k, :]), (own_h[:, q, c], W1l[:, 1, k, :]),
                                             (own_l[:, q, c], W1h[:, 1, k, :])]
                            mm = accumulate(pe, bank[2 + u // 2][:, (u % 2) * H:(u % 2 + 1) * H], products)
                        mm.then_inc(dense, 1)

                    def turn(b, s, i):
                        pe.wait_ge(own_in[s], 16 * (i + 1))
                        wait(pe, lo, K * b)
                        for k in range(K):
                            for u in range(U):
                                mm = pe.transpose(bank[k][:, u * P:(u + 1) * P],
                                                  own[:, s, u * H + k * P:u * H + (k + 1) * P], ident[:, :])
                        mm.then_inc(turned, 1)

                    def product_2(b, s, i):
                        q = s % 2
                        pe.wait_ge(h2_lo, K * (b + 1))
                        wait(pe, s_out, b)
                        for u in range(U):
                            products = []
                            for k in range(K):
                                c = slice(k * 512 + u * P, k * 512 + (u + 1) * P)
                                products += [(h2_h[:, q, c], Wr2_r[:, k, :]), (h2_l[:, q, c], Wr2_r[:, k, :])]
                            mm = accumulate(pe, bank[6 + u // 2][:, (u % 2) * H:(u % 2 + 1) * H], products)
                        mm.then_inc(dense2, 1)

                    def turn_r(b, s, i):
                        pe.wait_ge(r_ready, b + 1)
                        wait(pe, h2_lo, K * b)
                        for k in range(K):
                            for u in range(U):
                                mm = pe.transpose(bank[4 + k][:, u * P:(u + 1) * P],
                                                  res[:, s % 2, u * H + k * P:u * H + (k + 1) * P], ident[:, :])
                        mm.then_inc(r_turned, 1)

                    lagged(pe, (2, product), (0, turn), (3, product_2), (2, turn_r))

                @block.vector
                def _(dve):
                    def lower(b, s, i):
                        wait(dve, dense, b - 1)
                        for k in range(K):
                            dve.wait_ge(hi, K * b + k + 1)
                            c = slice(k * 512, (k + 1) * 512)
                            dve.tensor_tensor(own_l[:, s % 2, c], bank[k][:, :], own_h[:, s % 2, c].bitcast(F32),
                                              ALU.subtract).then_inc(lo, 1)

                    def lower_h2(b, s, i):
                        wait(dve, dense2, b - 1)
                        for k in range(K):
                            dve.wait_ge(h2_hi, K * b + k + 1)
                            c = slice(k * 512, (k + 1) * 512)
                            dve.scalar_tensor_tensor(h2_l[:, s % 2, c], bank[4 + k][:, :], 0.0,
                                                     h2_h[:, s % 2, c].bitcast(F32), ALU.max, ALU.subtract)\
                                .then_inc(h2_lo, 1)

                    def combine(b, s, i):
                        q = s % 2
                        dve.wait_ge(gathered[s], gathers(nth, s, i + 1))
                        dve.wait_ge(dense, b + 1)
                        wait(dve, r_turned, b - 1)
                        wait(dve, stored_r[q], 16 * uses(s, i))
                        for u in range(U):
                            c = slice(u * H, (u + 1) * H)
                            last = dve.scalar_tensor_tensor(
                                res[:, q, c], raw[:, s, c], node_inv[:, at(b), u:u + 1].rearrange("p a u -> p (a u)"),
                                bank[2 + u // 2][:, (u % 2) * H:(u % 2 + 1) * H], ALU.mult, ALU.add)
                        last.then_inc(r_ready, 1)

                    def half_product(n, g):
                        return bank[6 + n][:, :].rearrange("p (u g d) -> p u g d", u=2, g=2)[:, :, g, :]

                    def residual(b, s, i):
                        dve.wait_ge(x_in[s], 16 * (i + 1))
                        dve.wait_ge(dense2, b + 1)
                        for n in range(2):
                            x_rows = x1_b[:, s, n * 2 * D:(n + 1) * 2 * D].rearrange("p (u d) -> p u d", u=2)
                            last = dve.tensor_tensor(x_rows, half_product(n, 0), x_rows, ALU.add)
                        last.then_inc(half_added, 1)

                    def residual_2(b, s, i):
                        q = s % 2
                        dve.wait_ge(half_added, b + 1)
                        wait(dve, stored_s[q], 16 * uses(s, i))
                        for n in range(2):
                            c = slice(n * 2 * D, (n + 1) * 2 * D)
                            last = dve.tensor_tensor(res2[:, q, c].rearrange("p (u d) -> p u d", u=2),
                                                     half_product(n, 1),
                                                     x1_b[:, s, c].rearrange("p (u d) -> p u d", u=2), ALU.add)
                        last.then_inc(s_out, 1)

                    lagged(dve, (4, residual), (1, lower), (4, residual_2), (3, lower_h2), (2, combine))

                @block.scalar
                def _(act):
                    def upper_h2(b, s, i):
                        act.wait_ge(r_turned, b + 1)
                        wait(act, dense2, b - 1)
                        for k in range(K):
                            act.activation(h2_h[:, s % 2, k * 512:(k + 1) * 512], bank[4 + k][:, :], ACT.Relu)\
                                .then_inc(h2_hi, 1)

                    def store_r(b, s, i):
                        act.wait_ge(r_ready, b + 1)
                        act.dma_start(rows_of(h2_t, b), res[:, s % 2, :]).then_inc(stored_r[s % 2], 16)

                    def upper(b, s, i):
                        act.wait_ge(turned, b + 1)
                        wait(act, dense, b - 1)
                        for k in range(K):
                            act.activation(own_h[:, s % 2, k * 512:(k + 1) * 512], bank[k][:, :], ACT.Copy)\
                                .then_inc(hi, 1)

                    def store_s(b, s, i):
                        act.wait_ge(s_out, b + 1)
                        act.dma_start(rows_of(s2_t, b), res2[:, s % 2, 0:U * D]).then_inc(stored_s[s % 2], 16)

                    lagged(act, (3, upper_h2), (3, store_r), (0, upper), (4, store_s))
                    for s in range(2):
                        act.wait_ge(stored_r[s], 16 * (NB // 2))
                        act.wait_ge(stored_s[s], 16 * (NB // 2))

        def sage_2(nth):
            s_in = [sem(f"b2_s_in{s}") for s in range(R)]
            stored = [sem(f"b2_stored{s}") for s in range(2)]
            x_stored = [sem(f"b2_x_stored{s}") for s in range(R)]
            step = sem("b2_step")
            x1_ready = sem("b2_x1")
            mean_var = sem("b2_mean_var")
            std_ready = sem("b2_std")
            rstd_ready = sem("b2_rstd")
            h_ready = sem("b2_h")
            turned = sem("b2_turned")
            hi = sem("b2_hi")
            lo = sem("b2_lo")
            dense = sem("b2_dense")
            y_act = sem("b2_y_act")
            y_dve = sem("b2_y_dve")
            with nc.Block() as block:

                @block.gpsimd
                def _(pool):
                    gather_blocks(pool, pa_t, node_row, D, nth, x1_ready)

                @block.sync
                def _(sp):
                    def load(b, s, i):
                        wait(sp, x1_ready, b - R + 1)
                        sp.dma_start(own[:, s, 0:U * D], rows_of(s2_t, b)).then_inc(s_in[s], 16)

                    def store_x1(b, s, i):
                        sp.wait_ge(x1_ready, b + 1)
                        sp.dma_start(rows_of(x1_t, b), x1_b[:, s, :]).then_inc(x_stored[s], 16)

                    lagged(sp, (0, load), (2, store_x1))
                    for s in range(R):
                        sp.wait_ge(x_stored[s], 16 * in_pass(s))

                @block.vector
                def _(dve):
                    def residual(b, s, i):
                        dve.wait_ge(s_in[s], 16 * (i + 1))
                        dve.wait_ge(gathered[s], gathers(nth, s, i + 1))
                        wait(dve, x_stored[s], 16 * i)
                        wait(dve, h_ready, b - R + 1)
                        for u in range(U):
                            c = slice(u * D, (u + 1) * D)
                            last = dve.scalar_tensor_tensor(
                                x1_b[:, s, c], raw[:, s, c], node_inv[:, at(b), u:u + 1].rearrange("p a u -> p (a u)"),
                                own[:, s, c], ALU.mult, ALU.add)
                        last.then_inc(x1_ready, 1)
                        dve.wait_ge(x1_ready, b + 1)
                        rows = x1_b[:, s, :].rearrange("p (u d) -> p u d", u=U)
                        ln_stats(dve, rows, s, step, U * b).then_inc(mean_var, 1)

                    def scalars(b, s, i):
                        ln_scalars(dve, s, b, std_ready, rstd_ready)

                    def lower(b, s, i):
                        q = s % 2
                        dve.wait_ge(hi, b + 1)
                        wait(dve, dense, U * (b - 1))
                        dve.tensor_tensor(big_l[:, q, 0:512], bank[q][:, :], big_h[:, q, 0:512].bitcast(F32),
                                          ALU.subtract).then_inc(lo, 1)

                    def evacuate(b, s, i):
                        q = s % 2
                        dve.wait_ge(dense, U * (b + 1))
                        wait(dve, stored[q], 48 * uses(s, i))
                        y = res2[:, q, :].rearrange("p (n u d) -> p n u d", n=3, u=U)
                        dve.tensor_copy(y[:, :, U - 1, :], bank[2 + U - 1][:, 0:3 * D].rearrange(
                            "p (n d) -> p n d", n=3)).then_inc(y_dve, 1)

                    lagged(dve, (1, scalars), (2, lower), (0, residual), (3, evacuate))

                @block.scalar
                def _(act):
                    def deviation(b, s, i):
                        act.wait_ge(mean_var, b + 1)
                        act.activation(std[:, s, :], mv[:, s, :, 1], ACT.Sqrt, bias=eps_c[:, 0:1])\
                            .then_inc(std_ready, 1)

                    def apply(b, s, i):
                        act.wait_ge(rstd_ready, 2 * b + 2)
                        wait(act, turned, b - 1)
                        for u in range(U):
                            last = act.activation(h3_b[:, s % 2, u * D:(u + 1) * D], x1_b[:, s, u * D:(u + 1) * D],
                                                  ACT.Relu, bias=nbias[:, s, u:u + 1], scale=rstd[:, s, u:u + 1])
                        last.then_inc(h_ready, 1)

                    def upper(b, s, i):
                        act.wait_ge(turned, b + 1)
                        wait(act, dense, U * (b - 1))
                        act.activation(big_h[:, s % 2, 0:512], bank[s % 2][:, :], ACT.Copy).then_inc(hi, 1)

                    def evacuate(b, s, i):
                        q = s % 2
                        wait(act, stored[q], 48 * uses(s, i))
                        y = res2[:, q, :].rearrange("p (n u d) -> p n u d", n=3, u=U)
                        for u in range(U - 1):
                            act.wait_ge(dense, U * b + u + 1)
                            act.activation(y[:, :, u, :], bank[2 + u][:, 0:3 * D].rearrange(
                                "p (n d) -> p n d", n=3), ACT.Copy).then_inc(y_act, 1)

                    def store(b, s, i):
                        act.wait_ge(y_act, (U - 1) * (b + 1))
                        act.wait_ge(y_dve, b + 1)
                        for n, t in enumerate((y_t[0:NP, :], y_t[NP:2 * NP, :], self_t)):
                            act.dma_start(rows_of(t, b), res2[:, s % 2, n * U * D:(n + 1) * U * D])\
                                .then_inc(stored[s % 2], 16)

                    lagged(act, (2, upper), (1, apply), (3, evacuate), (0, deviation), (4, store))
                    for s in range(2):
                        act.wait_ge(stored[s], 48 * (NB // 2))

                @block.tensor
                def _(pe):
                    def turn(b, s, i):
                        pe.wait_ge(h_ready, b + 1)
                        wait(pe, lo, b - 1)
                        for u in range(U):
                            mm = pe.transpose(bank[s % 2][:, u * P:(u + 1) * P], h3_b[:, s % 2, u * D:(u + 1) * D],
                                              ident[:, :])
                        mm.then_inc(turned, 1)

                    def product(b, s, i):
                        q = s % 2
                        pe.wait_ge(lo, b + 1)
                        for u in range(U):
                            if u < U - 1:
                                wait(pe, y_act, (U - 1) * (b - 1) + u + 1)
                            else:
                                wait(pe, y_dve, b)
                            c = slice(u * P, (u + 1) * P)
                            accumulate(pe, bank[2 + u][:, 0:3 * D], [
                                (ones_r[:, :], bias3),
                                (big_h[:, q, c], W3h[:, :]), (big_h[:, q, c], W3l[:, :]),
                                (big_l[:, q, c], W3h[:, :])]).then_inc(dense, 1)

                    lagged(pe, (0, turn), (1, product))

        def relational(nth):
            x_in = [sem(f"b3_x_in{s}") for s in range(R)]
            stored = [sem(f"b3_stored{s}") for s in range(2)]
            added = sem("b3_added")
            relu_done = sem("b3_relu")
            o_ready = sem("b3_out")
            with nc.Block() as block:

                @block.gpsimd
                def _(pool):
                    gather_blocks(pool, pa_t, node_row, D, nth, added)

                @block.sync
                def _(sp):
                    def load(b, s, i):
                        wait(sp, o_ready, b - R + 1)
                        sp.dma_start(own[:, s, 0:U * D], rows_of(self_t, b)).then_inc(x_in[s], 16)
                        sp.dma_start(own[:, s, U * D:2 * U * D], rows_of(x1_t, b)).then_inc(x_in[s], 16)

                    lagged(sp, (0, load))

                @block.vector
                def _(dve):
                    def add_self(b, s, i):
                        dve.wait_ge(x_in[s], 32 * (i + 1))
                        dve.wait_ge(gathered[s], gathers(nth, s, i + 1))
                        wait(dve, relu_done, b - 1)
                        dve.tensor_tensor(res2[:, s % 2, 0:U * D], raw[:, s, 0:U * D], own[:, s, 0:U * D], ALU.add)\
                            .then_inc(added, 1)

                    def residual(b, s, i):
                        q = s % 2
                        dve.wait_ge(relu_done, b + 1)
                        if not isinstance(b, int) or b - 2 <= FULL:
                            wait(dve, stored[q], 16 * uses(s, i))
                        dve.tensor_tensor(res[:, q, U * D:2 * U * D], res[:, q, 0:U * D], own[:, s, U * D:2 * U * D],
                                          ALU.add).then_inc(o_ready, 1)

                    lagged(dve, (0, add_self), (1, residual))

                @block.scalar
                def _(act):
                    def relu(b, s, i):
                        act.wait_ge(added, b + 1)
                        wait(act, o_ready, b - 1)
                        act.activation(res[:, s % 2, 0:U * D], res2[:, s % 2, 0:U * D], ACT.Relu).then_inc(relu_done, 1)

                    def store(b, s, i):
                        act.wait_ge(o_ready, b + 1)
                        q = s % 2
                        if isinstance(b, int) and b > FULL:
                            return
                        if isinstance(b, int) and b == FULL:
                            act.dma_start(out[b * BLK:N, :].rearrange("(p u) d -> p (u d)", u=U),
                                          res[0:TAIL, q, U * D:2 * U * D]).then_inc(stored[q], 16)
                        else:
                            act.dma_start(rows_of(out, b), res[:, q, U * D:2 * U * D]).then_inc(stored[q], 16)

                    lagged(act, (0, relu), (2, store))
                    for s in range(2):
                        act.wait_ge(stored[s], 16 * len(range(s, FULL + 1, 2)))

        with ExitStack() as scratch:
            run(prepare, scratch)

        stage = sb("stage", [P, R, U], I32)
        raw = sb("raw", [P, R, U * H])
        own = sb("own", [P, R, U * H])
        big_h = sb("big_h", [P, 2, U * H], F32R)
        big_l = sb("big_l", [P, 2, U * H], F32R)
        own_h = sb("own_h", [P, 2, U * H], F32R)
        own_l = sb("own_l", [P, 2, U * H], F32R)
        S = sb("S", [P, 2, U, P], F32R)
        res = sb("res", [P, 2, U * H])
        res2 = sb("res2", [P, 2, U * 3 * D])
        x1_b = sb("x1_b", [P, R, U * D])
        h3_b = sb("h3_b", [P, 2, U * D])
        stats = sb("stats", [P, R, U, 6])
        mv = sb("mv", [P, R, U, 2])
        std = sb("std", [P, R, U])
        rstd = sb("rstd", [P, R, U])
        nbias = sb("nbias", [P, R, U])
        pay_stage = sb("pay_stage", [P, R, 2 * U])
        half = sb("half", [P, 2, U, D])
        h2_h = sb("h2_h", [P, 2, U * H], F32R)
        h2_l = sb("h2_l", [P, 2, U * H], F32R)

        run(layer_norm_x)
        run(load_node_entries)
        run(run_sums, "a0", 0, D, h0_t, src_T, pa_t)
        run(carry_runs, 0, D, pa_t)
        run(sage_0, 1)
        run(transformed_sums, "a1", 2, h1_t, src_T, W1h[:, 0, :, :], W1l[:, 0, :, :], pb_t, False)
        run(carry_runs, 1, H, pb_t)
        run(sage_1, 3)
        run(transformed_sums, "a2", 4, h2_t, src_T, Wl2_r[:, :, :], None, pa_t, True)
        run(carry_runs, 2, D, pa_t)
        run(sage_2, 5)
        run(run_sums, "a3", 6, D, y_t, srcy_T, pa_t)
        run(carry_runs, 3, D, pa_t)
        run(relational, 7)


INPUTS = ["x", "src", "dst", "edge_type_2", "L0_gnn_Wl0", "L0_gnn_b0", "L0_gnn_Wr0", "L0_gnn_Wl1", "L0_gnn_b1",
          "L0_gnn_Wr1", "L0_gnn_Wl2", "L0_gnn_b2", "L0_gnn_Wr2", "L1_gnn_W_data", "L1_gnn_b_data",
          "L1_gnn_W_control", "L1_gnn_b_control", "L1_gnn_W_self", "L1_gnn_b_self"]


def kernel(**inputs):
    import numpy as np
    import concourse.bacc as bacc
    from concourse.bass_utils import run_bass_kernel_spmd

    nc = bacc.Bacc("TRN2", target_bir_lowering=False, num_devices=1)
    arrays, args = {}, []
    for name in INPUTS:
        a = np.ascontiguousarray(inputs[name])
        arrays["in_" + name] = a
        args.append(nc.dram_tensor("in_" + name, a.shape, mybir.dt.from_np(a.dtype), kind="ExternalInput").ap())
    out = nc.dram_tensor("out", inputs["x"].shape, F32, kind="ExternalOutput").ap()
    build(nc, *args, out)
    return run_bass_kernel_spmd(nc, [arrays], core_ids=[0]).results[0]["out"]
```
